# Optimizing a Trainium2 kernel written in Bass

```python
import numpy as np
import jax
import jax.numpy as jnp

def _softmax(x, axis=-1):
    return jax.nn.softmax(x, axis=axis)

def _gelu(x):
    return jax.nn.gelu(x, approximate=True)

def _silu(x):
    return jax.nn.silu(x)

def _sigmoid(x):
    return jax.nn.sigmoid(x)

def _layernorm(x, axis=-1, eps=1e-05):
    m = jnp.mean(x, axis=axis, keepdims=True)
    v = jnp.var(x, axis=axis, keepdims=True)
    return (x - m) / jnp.sqrt(v + eps)

def _scatter_add(tgt, idx, src, axis=0):
    return tgt.at[idx].add(src)

def _segment_sum(src, seg, n):
    return jax.ops.segment_sum(src, seg, n)
kernel_name = 'mk_decoder_postln_d1_seqx_r4_3a8886'

def setup_inputs(seed: int=0):
    np.random.seed(seed)
    _w = jnp.asarray

    def _rec_inputs():
        import jax
        import jax.numpy as jnp
        _rk = jax.random.key(seed)
        x = 7.22e-05 + 1 * jax.random.normal(jax.random.fold_in(_rk, 1), (8, 256, 512), jnp.float32)
        _lenS = 256 - jax.random.randint(jax.random.fold_in(_rk, 7), (8,), 0, max(1, 256 // 4) + 1, jnp.int32)
        _lenS2 = 256 - jax.random.randint(jax.random.fold_in(_rk, 8), (8,), 0, max(1, 256 // 4) + 1, jnp.int32)
        _ctx_2048P = jax.random.normal(jax.random.fold_in(_rk, 12), (8, 16, 512), jnp.float32)
        _ctx_2048c = jax.random.dirichlet(jax.random.fold_in(_rk, 512), 0.3 * jnp.ones((16,), jnp.float32), (8, 256))
        _ctx_2048t = jnp.einsum('bsk,bkd->bsd', _ctx_2048c, _ctx_2048P)
        _ctx_2048t = _ctx_2048t * jax.lax.rsqrt(jnp.mean(jnp.square(_ctx_2048t)) + 1e-12) * 0.953939
        ctx_2048 = 0.00424091 + 1.0017 * (_ctx_2048t + 0.3 * jax.random.normal(jax.random.fold_in(_rk, 612), (8, 256, 512), jnp.float32))
        _validS = jnp.arange(256)[None, :] < _lenS[:, None]
        _validS2 = jnp.arange(256)[None, :] < _lenS2[:, None]
        _causal = jnp.tril(jnp.ones((256, 256), dtype=bool))
        mask_Bx1xSxS_fk0 = jnp.where(jnp.broadcast_to(_validS[:, None, None, :], (8, 1, 256, 256)), -1000000000.0, 0.0).astype(jnp.float32)
        return (x, ctx_2048, mask_Bx1xSxS_fk0)
    x, ctx_2048, mask_Bx1xSxS_fk0 = _rec_inputs()

    def _L0_attn_setup():
        import jax, jax.numpy as jnp
        import numpy as np
        B, S, D_IN = (1, 256, 512)
        H_QK, H_V, DK, DV = (8, 16, 128, 128)
        KCONV = 4
        D_OUT = H_QK * DK
        D_OUT_VG = H_V * DV
        FUSED = 2 * D_OUT + D_OUT_VG
        EPS = 1e-06

        def l2_norm(t):
            return t / jnp.sqrt(jnp.sum(t * t, axis=-1, keepdims=True) + EPS)

        def rms_norm(t, w):
            var = jnp.mean(t * t, axis=-1, keepdims=True)
            return t * jax.lax.rsqrt(var + EPS) * w

        def gated_delta_rule(q, k, v, beta, alpha):
            q = q * q.shape[-1] ** (-0.5)
            S0 = jnp.zeros(q.shape[:2] + (q.shape[-1], v.shape[-1]), q.dtype)

            def step(Sm, inp):
                q_t, k_t, v_t, b_t, a_t = inp
                Sm = Sm * a_t[..., None, None]
                kv = jnp.einsum('bhk,bhkv->bhv', k_t, Sm)
                u = (v_t - kv) * b_t[..., None]
                Sm = Sm + k_t[..., None] * u[:, :, None, :]
                o = jnp.einsum('bhk,bhkv->bhv', q_t, Sm)
                return (Sm, o)
            xs = (jnp.moveaxis(q, 2, 0), jnp.moveaxis(k, 2, 0), jnp.moveaxis(v, 2, 0), jnp.moveaxis(beta, 2, 0), jnp.moveaxis(alpha, 2, 0))
            Sf, outs = jax.lax.scan(step, S0, xs)
            return (jnp.moveaxis(outs, 0, 2), Sf)
        key = jax.random.key(seed)
        ks = jax.random.split(key, 8)
        return {'x': jax.random.normal(ks[0], (B, S, D_IN), jnp.float32), 'w_qkv': jax.random.normal(ks[1], (FUSED, D_IN), jnp.float32) * 0.02, 'w_gate': jax.random.normal(ks[2], (D_OUT_VG, D_IN), jnp.float32) * 0.02, 'w_beta': jax.random.normal(ks[3], (H_V, D_IN), jnp.float32) * 0.02, 'w_alpha': jax.random.normal(ks[4], (H_V, D_IN), jnp.float32) * 0.02, 'log_A': jnp.log(jax.random.uniform(ks[5], (H_V,), jnp.float32, 0.001, 16.0)), 'dt_bias': jnp.ones((H_V,), jnp.float32), 'conv_w': jax.random.normal(ks[6], (FUSED, 1, KCONV), jnp.float32) * 0.1, 'rms_w': jnp.ones((DV,), jnp.float32), 'w_out': jax.random.normal(ks[7], (D_IN, D_OUT_VG), jnp.float32) * 0.02}
    _L0_attn_all = _L0_attn_setup()
    _L0_attn_in = {k: v for k, v in _L0_attn_all.items() if k in ('w_qkv', 'w_gate', 'w_beta', 'w_alpha', 'log_A', 'dt_bias', 'conv_w', 'rms_w', 'w_out')}
    del _L0_attn_all

    def _L0_xattn_setup():
        import jax, jax.numpy as jnp
        import numpy as np
        import math
        B, S, HID, H = (2, 512, 512, 32)
        D = HID // H
        AL = 10

        def _rope_tables(seq_len, dim, dtype):
            inv_freq = 1.0 / 10000.0 ** (np.arange(0, dim, 2, dtype=np.float32) / dim)
            t = np.arange(seq_len, dtype=np.float32)
            freqs = np.outer(t, inv_freq)
            emb = np.concatenate([freqs, freqs], -1)
            return (jnp.asarray(np.cos(emb), dtype), jnp.asarray(np.sin(emb), dtype))

        def _rotate_half(x):
            x1, x2 = jnp.split(x, 2, axis=-1)
            return jnp.concatenate([-x2, x1], axis=-1)
        key = jax.random.key(seed)
        ks = jax.random.split(key, 8)
        hidden_states = jax.random.normal(ks[0], (B, S, HID), dtype=jnp.float32)
        adapter = jax.random.normal(ks[1], (B, AL, HID), dtype=jnp.float32)
        causal = jnp.tril(jnp.ones((S, S), dtype=bool))
        attention_mask = jnp.broadcast_to(jnp.where(causal, 0.0, -1000000000.0).astype(jnp.float32)[None, None], (B, 1, S, S))
        scale = 0.02
        Wq = jax.random.normal(ks[2], (HID, HID), dtype=jnp.float32) * scale
        Wk = jax.random.normal(ks[3], (HID, HID), dtype=jnp.float32) * scale
        Wv = jax.random.normal(ks[4], (HID, HID), dtype=jnp.float32) * scale
        Wo = jax.random.normal(ks[5], (HID, HID), dtype=jnp.float32) * scale
        gate = jax.random.normal(ks[6], (1, H, 1, 1), dtype=jnp.float32) * 0.1
        return {'hidden_states': hidden_states, 'attention_mask': attention_mask, 'adapter': adapter, 'Wq': Wq, 'Wk': Wk, 'Wv': Wv, 'Wo': Wo, 'gate': gate}
    _L0_xattn_all = _L0_xattn_setup()
    _L0_xattn_in = {k: v for k, v in _L0_xattn_all.items() if k in ('Wq', 'Wk', 'Wv', 'Wo', 'gate')}
    del _L0_xattn_all

    def _L0_ffn_setup():
        import jax, jax.numpy as jnp
        import numpy as np
        CAPACITY = 0.125
        HEAD_DIM = 128
        N_HEADS = 16
        N_KV_HEADS = 8
        ROPE_THETA = 10000.0
        EPS = 1e-06

        def _rms_norm(x, w):
            return x * jax.lax.rsqrt(jnp.mean(x * x, axis=-1, keepdims=True) + EPS) * w

        def _rotate_half(t):
            h = t.shape[-1] // 2
            return jnp.concatenate([-t[..., h:], t[..., :h]], axis=-1)
        key = jax.random.key(seed)
        ks = jax.random.split(key, 12)
        B, T, D = (4, 1024, 512)
        I = 2048
        s = 0.02
        return {'hidden_states': jax.random.normal(ks[0], (B, T, D), jnp.float32), 'w_router': jax.random.normal(ks[1], (D,), jnp.float32) * s, 'wq': jax.random.normal(ks[2], (D, N_HEADS * HEAD_DIM), jnp.float32) * s, 'bq': jnp.zeros((N_HEADS * HEAD_DIM,), jnp.float32), 'wk': jax.random.normal(ks[3], (D, N_KV_HEADS * HEAD_DIM), jnp.float32) * s, 'bk': jnp.zeros((N_KV_HEADS * HEAD_DIM,), jnp.float32), 'wv': jax.random.normal(ks[4], (D, N_KV_HEADS * HEAD_DIM), jnp.float32) * s, 'bv': jnp.zeros((N_KV_HEADS * HEAD_DIM,), jnp.float32), 'wo': jax.random.normal(ks[5], (N_HEADS * HEAD_DIM, D), jnp.float32) * s, 'w_gate': jax.random.normal(ks[6], (D, I), jnp.float32) * s, 'w_up': jax.random.normal(ks[7], (D, I), jnp.float32) * s, 'w_down': jax.random.normal(ks[8], (I, D), jnp.float32) * s, 'ln1_w': jnp.ones((D,), jnp.float32), 'ln2_w': jnp.ones((D,), jnp.float32)}
    _L0_ffn_all = _L0_ffn_setup()
    _L0_ffn_in = {k: v for k, v in _L0_ffn_all.items() if k in ('w_router', 'wq', 'bq', 'wk', 'bk', 'wv', 'bv', 'wo', 'w_gate', 'w_up', 'w_down', 'ln1_w', 'ln2_w')}
    del _L0_ffn_all
    return {'x': x, 'ctx_2048': ctx_2048, 'mask_Bx1xSxS_fk0': mask_Bx1xSxS_fk0, 'L0_attn_w_qkv': _L0_attn_in['w_qkv'], 'L0_attn_w_gate': _L0_attn_in['w_gate'], 'L0_attn_w_beta': _L0_attn_in['w_beta'], 'L0_attn_w_alpha': _L0_attn_in['w_alpha'], 'L0_attn_log_A': _L0_attn_in['log_A'], 'L0_attn_dt_bias': _L0_attn_in['dt_bias'], 'L0_attn_conv_w': _L0_attn_in['conv_w'], 'L0_attn_rms_w': _L0_attn_in['rms_w'], 'L0_attn_w_out': _L0_attn_in['w_out'], 'L0_xattn_Wq': _L0_xattn_in['Wq'], 'L0_xattn_Wk': _L0_xattn_in['Wk'], 'L0_xattn_Wv': _L0_xattn_in['Wv'], 'L0_xattn_Wo': _L0_xattn_in['Wo'], 'L0_xattn_gate': _L0_xattn_in['gate'], 'L0_ffn_w_router': _L0_ffn_in['w_router'], 'L0_ffn_wq': _L0_ffn_in['wq'], 'L0_ffn_bq': _L0_ffn_in['bq'], 'L0_ffn_wk': _L0_ffn_in['wk'], 'L0_ffn_bk': _L0_ffn_in['bk'], 'L0_ffn_wv': _L0_ffn_in['wv'], 'L0_ffn_bv': _L0_ffn_in['bv'], 'L0_ffn_wo': _L0_ffn_in['wo'], 'L0_ffn_w_gate': _L0_ffn_in['w_gate'], 'L0_ffn_w_up': _L0_ffn_in['w_up'], 'L0_ffn_w_down': _L0_ffn_in['w_down'], 'L0_ffn_ln1_w': _L0_ffn_in['ln1_w'], 'L0_ffn_ln2_w': _L0_ffn_in['ln2_w']}

def reference(x, ctx_2048, mask_Bx1xSxS_fk0, L0_attn_w_qkv, L0_attn_w_gate, L0_attn_w_beta, L0_attn_w_alpha, L0_attn_log_A, L0_attn_dt_bias, L0_attn_conv_w, L0_attn_rms_w, L0_attn_w_out, L0_xattn_Wq, L0_xattn_Wk, L0_xattn_Wv, L0_xattn_Wo, L0_xattn_gate, L0_ffn_w_router, L0_ffn_wq, L0_ffn_bq, L0_ffn_wk, L0_ffn_bk, L0_ffn_wv, L0_ffn_bv, L0_ffn_wo, L0_ffn_w_gate, L0_ffn_w_up, L0_ffn_w_down, L0_ffn_ln1_w, L0_ffn_ln2_w):
    import jax
    import jax.numpy as jnp

    def _L0_attn_ref(x, w_qkv, w_gate, w_beta, w_alpha, log_A, dt_bias, conv_w, rms_w, w_out):
        import jax, jax.numpy as jnp
        import numpy as np
        B, S, D_IN = (1, 256, 512)
        H_QK, H_V, DK, DV = (8, 16, 128, 128)
        KCONV = 4
        D_OUT = H_QK * DK
        D_OUT_VG = H_V * DV
        FUSED = 2 * D_OUT + D_OUT_VG
        EPS = 1e-06

        def l2_norm(t):
            return t / jnp.sqrt(jnp.sum(t * t, axis=-1, keepdims=True) + EPS)

        def rms_norm(t, w):
            var = jnp.mean(t * t, axis=-1, keepdims=True)
            return t * jax.lax.rsqrt(var + EPS) * w

        def gated_delta_rule(q, k, v, beta, alpha):
            q = q * q.shape[-1] ** (-0.5)
            S0 = jnp.zeros(q.shape[:2] + (q.shape[-1], v.shape[-1]), q.dtype)

            def step(Sm, inp):
                q_t, k_t, v_t, b_t, a_t = inp
                Sm = Sm * a_t[..., None, None]
                kv = jnp.einsum('bhk,bhkv->bhv', k_t, Sm)
                u = (v_t - kv) * b_t[..., None]
                Sm = Sm + k_t[..., None] * u[:, :, None, :]
                o = jnp.einsum('bhk,bhkv->bhv', q_t, Sm)
                return (Sm, o)
            xs = (jnp.moveaxis(q, 2, 0), jnp.moveaxis(k, 2, 0), jnp.moveaxis(v, 2, 0), jnp.moveaxis(beta, 2, 0), jnp.moveaxis(alpha, 2, 0))
            Sf, outs = jax.lax.scan(step, S0, xs)
            return (jnp.moveaxis(outs, 0, 2), Sf)
        b, seq_len, _ = x.shape
        fused_qkv = x @ w_qkv.T
        beta = jax.nn.sigmoid(x @ w_beta.T).transpose(0, 2, 1)
        token_projs = x @ w_alpha.T
        alpha = jnp.exp(-jnp.exp(log_A) * jax.nn.softplus(token_projs + dt_bias))
        alpha = alpha.transpose(0, 2, 1)
        conv_in = fused_qkv.transpose(0, 2, 1)
        conv_out = jax.lax.conv_general_dilated(conv_in, conv_w, window_strides=(1,), padding=[(KCONV - 1, 0)], dimension_numbers=('NCH', 'OIH', 'NCH'), feature_group_count=FUSED)
        fused_qkv = jax.nn.silu(conv_out).transpose(0, 2, 1)
        query = fused_qkv[..., :D_OUT].reshape(b, seq_len, H_QK, DK).transpose(0, 2, 1, 3)
        key = fused_qkv[..., D_OUT:2 * D_OUT].reshape(b, seq_len, H_QK, DK).transpose(0, 2, 1, 3)
        value = fused_qkv[..., 2 * D_OUT:].reshape(b, seq_len, H_V, DV).transpose(0, 2, 1, 3)
        query, key = (l2_norm(query), l2_norm(key))
        rep = H_V // H_QK
        if rep > 1:
            query = jnp.repeat(query, rep, axis=1)
            key = jnp.repeat(key, rep, axis=1)
        ctx, _ = gated_delta_rule(query, key, value, beta, alpha)
        ctx = rms_norm(ctx.astype(jnp.float32), rms_w)
        ctx = ctx.transpose(0, 2, 1, 3).reshape(b, seq_len, D_OUT_VG)
        gate = jax.nn.silu(x @ w_gate.T)
        return gate * ctx @ w_out.T

    def _L0_xattn_ref(hidden_states, attention_mask, adapter, Wq, Wk, Wv, Wo, gate):
        import jax, jax.numpy as jnp
        import numpy as np
        import math
        B, S, HID, H = (2, 512, 512, 32)
        D = HID // H
        AL = 10

        def _rope_tables(seq_len, dim, dtype):
            inv_freq = 1.0 / 10000.0 ** (np.arange(0, dim, 2, dtype=np.float32) / dim)
            t = np.arange(seq_len, dtype=np.float32)
            freqs = np.outer(t, inv_freq)
            emb = np.concatenate([freqs, freqs], -1)
            return (jnp.asarray(np.cos(emb), dtype), jnp.asarray(np.sin(emb), dtype))

        def _rotate_half(x):
            x1, x2 = jnp.split(x, 2, axis=-1)
            return jnp.concatenate([-x2, x1], axis=-1)
        bsz, q_len, hid = hidden_states.shape
        n_heads = gate.shape[1]
        head_dim = hid // n_heads
        inv_sqrt_d = 1.0 / math.sqrt(head_dim)

        def split_heads(x, length):
            return x.reshape(bsz, length, n_heads, head_dim).transpose(0, 2, 1, 3)
        q = split_heads(hidden_states @ Wq, q_len)
        k = split_heads(hidden_states @ Wk, q_len)
        v = split_heads(hidden_states @ Wv, q_len)
        cos, sin = _rope_tables(q_len, head_dim, q.dtype)
        q = q * cos + _rotate_half(q) * sin
        k = k * cos + _rotate_half(k) * sin
        scores = jnp.einsum('bhqd,bhkd->bhqk', q, k) * inv_sqrt_d
        scores = scores + attention_mask
        scores = jnp.maximum(scores, jnp.finfo(scores.dtype).min)
        w = jax.nn.softmax(scores.astype(jnp.float32), axis=-1).astype(q.dtype)
        attn_output = jnp.einsum('bhqk,bhkd->bhqd', w, v)
        adapter_len = adapter.shape[1]
        a_k = split_heads(adapter @ Wk, adapter_len)
        a_v = split_heads(adapter @ Wv, adapter_len)
        a_scores = jnp.einsum('bhqd,bhkd->bhqk', q, a_k) * inv_sqrt_d
        a_scores = jnp.tanh(gate) * jax.nn.softmax(a_scores.astype(jnp.float32), axis=-1).astype(q.dtype)
        attn_output = attn_output + jnp.einsum('bhqk,bhkd->bhqd', a_scores, a_v)
        attn_output = attn_output.transpose(0, 2, 1, 3).reshape(bsz, q_len, hid)
        return attn_output @ Wo

    def _L0_ffn_ref(hidden_states, w_router, wq, bq, wk, bk, wv, bv, wo, w_gate, w_up, w_down, ln1_w, ln2_w):
        import jax, jax.numpy as jnp
        import numpy as np
        CAPACITY = 0.125
        HEAD_DIM = 128
        N_HEADS = 16
        N_KV_HEADS = 8
        ROPE_THETA = 10000.0
        EPS = 1e-06

        def _rms_norm(x, w):
            return x * jax.lax.rsqrt(jnp.mean(x * x, axis=-1, keepdims=True) + EPS) * w

        def _rotate_half(t):
            h = t.shape[-1] // 2
            return jnp.concatenate([-t[..., h:], t[..., :h]], axis=-1)
        B, T, D = hidden_states.shape
        k = max(1, int(T * CAPACITY))
        scores = jnp.einsum('btd,d->bt', hidden_states, w_router)
        _, idx = jax.lax.top_k(scores, k)
        idx = jnp.sort(idx, axis=-1)
        b = jnp.arange(B)[:, None]
        sel = hidden_states[b, idx]
        sel_scores = scores[b, idx]
        S = B * k
        x = sel.reshape(S, D)
        pos = idx.reshape(S)
        inv_freq = 1.0 / ROPE_THETA ** (jnp.arange(0, HEAD_DIM, 2, dtype=jnp.float32) / HEAD_DIM)
        ang = pos.astype(jnp.float32)[:, None] * inv_freq
        cos = jnp.concatenate([jnp.cos(ang), jnp.cos(ang)], axis=-1)[:, None, :]
        sin = jnp.concatenate([jnp.sin(ang), jnp.sin(ang)], axis=-1)[:, None, :]
        h = _rms_norm(x, ln1_w)
        q = (h @ wq + bq).reshape(S, N_HEADS, HEAD_DIM)
        kk = (h @ wk + bk).reshape(S, N_KV_HEADS, HEAD_DIM)
        v = (h @ wv + bv).reshape(S, N_KV_HEADS, HEAD_DIM)
        q = q * cos + _rotate_half(q) * sin
        kk = kk * cos + _rotate_half(kk) * sin
        rep = N_HEADS // N_KV_HEADS
        kk = jnp.repeat(kk, rep, axis=1)
        v = jnp.repeat(v, rep, axis=1)
        att = jnp.einsum('shd,thd->hst', q, kk) / np.sqrt(HEAD_DIM)
        causal = jnp.tril(jnp.ones((S, S), bool))
        att = jnp.where(causal[None], att, jnp.finfo(att.dtype).min)
        att = jax.nn.softmax(att, axis=-1)
        attn_out = jnp.einsum('hst,thd->shd', att, v).reshape(S, N_HEADS * HEAD_DIM) @ wo
        x1 = x + attn_out
        h2 = _rms_norm(x1, ln2_w)
        mlp = jax.nn.silu(h2 @ w_gate) * (h2 @ w_up) @ w_down
        processed = x1 + mlp
        gate = jax.nn.sigmoid(sel_scores).reshape(S, 1)
        gated = gate * processed + (1.0 - gate) * x
        output = hidden_states.at[b, idx].set(gated.reshape(B, k, D))
        return output
    x = _layernorm(x + _L0_attn_ref(x, L0_attn_w_qkv, L0_attn_w_gate, L0_attn_w_beta, L0_attn_w_alpha, L0_attn_log_A, L0_attn_dt_bias, L0_attn_conv_w, L0_attn_rms_w, L0_attn_w_out), axis=-1)
    x = _layernorm(x + _L0_xattn_ref(x, mask_Bx1xSxS_fk0, ctx_2048, L0_xattn_Wq, L0_xattn_Wk, L0_xattn_Wv, L0_xattn_Wo, L0_xattn_gate), axis=-1)
    x = _layernorm(x + _L0_ffn_ref(x, L0_ffn_w_router, L0_ffn_wq, L0_ffn_bq, L0_ffn_wk, L0_ffn_bk, L0_ffn_wv, L0_ffn_bv, L0_ffn_wo, L0_ffn_w_gate, L0_ffn_w_up, L0_ffn_w_down, L0_ffn_ln1_w, L0_ffn_ln2_w), axis=-1)
    return x

_drawn_inputs = setup_inputs


def setup_inputs(seed=0):
    import zlib

    import numpy as np

    out = dict(_drawn_inputs(seed))
    spreads = {'L0_attn_dt_bias': (1.0, 0.6),
     'L0_attn_rms_w': (1.0, 0.6),
     'L0_ffn_bq': (0.0, 0.8),
     'L0_ffn_bk': (0.0, 0.8),
     'L0_ffn_bv': (0.0, 0.672),
     'L0_ffn_ln1_w': (1.0, 0.6),
     'L0_ffn_ln2_w': (1.0, 0.6)}
    factors = {'ctx_2048': 5.706,
     'L0_attn_w_beta': 6.542,
     'L0_attn_w_alpha': 8.0,
     'L0_attn_log_A': 3.536,
     'L0_xattn_Wq': 7.029,
     'L0_xattn_Wk': 7.059,
     'L0_xattn_gate': 4.493,
     'L0_ffn_w_router': 2.957,
     'L0_ffn_wq': 8.0,
     'L0_ffn_wk': 8.0,
     'L0_ffn_wv': 5.656,
     'L0_ffn_wo': 3.817,
     'L0_ffn_w_gate': 4.463,
     'L0_ffn_w_up': 4.36,
     'L0_ffn_w_down': 4.393}
    for name, (base, spread) in spreads.items():
        noise = np.random.default_rng([zlib.crc32(name.encode()), seed]).standard_normal(out[name].shape)
        drawn = base * np.exp(spread * noise) if base else spread * noise
        out[name] = jnp.asarray(drawn.astype(out[name].dtype))
    for name, factor in factors.items():
        out[name] = (out[name] * factor).astype(out[name].dtype)
    return out
```

```python
from contextlib import ExitStack

import numpy as np

import concourse.bass as bass
from concourse import mybir

F32 = mybir.dt.float32
ALU = mybir.AluOpType
ACT = mybir.ActivationFunctionType
AX_X = mybir.AxisListType.X

P = 128
B, S, D = 8, 256, 512
TOK = B * S
NT = TOK // P
KC = D // P

GH, VH = 8, 2
NH = GH * VH
NC = S // P
UNITS = GH * B
TAPS = 4
LEVELS = 7
DELTA_EPS = 1e-6
LN_EPS = 1e-5


def wait(engine, sem, value):
    if not isinstance(value, int) or value > 0:
        engine.wait_ge(sem, value)


class Space:

    def __init__(self, nc, stack, prefix):
        self.nc, self.stack, self.prefix, self.sems = nc, stack, prefix, []

    def sb(self, name, shape, dtype=F32):
        return self.stack.enter_context(self.nc.sbuf_tensor(self.prefix + name, shape, dtype))

    def bank(self, name):
        return self.stack.enter_context(self.nc.psum_tensor(self.prefix + name, [P, 512], F32))

    def sem(self, name):
        made = self.stack.enter_context(self.nc.semaphore(self.prefix + name))
        self.sems.append(made)
        return made

    def clear(self):
        with self.nc.Block() as block:

            @block.sync
            def _(sp):
                for used in self.sems:
                    sp.sem_clear(used)


def decay_phase(nc, x_t, w_ba, log_a, dt_bias, ident, beta_cols, alpha_dram):
    with ExitStack() as stack:
        a = Space(nc, stack, "dec_")
        w = a.sb("w", [P, KC, 2 * NH])
        la = a.sb("log_a", [P, NH])
        dt = a.sb("dt_bias", [P, NH])
        y = a.sb("y", [P, NT * NH])
        big = a.sb("big", [P, NT * NH])
        u = a.sb("u", [P, NT * NH])
        w1 = a.sb("w1", [P, NT * NH])
        poly = a.sb("poly", [P, NT * NH])
        small = a.sb("small", [P, NT * NH])
        neg_a = a.sb("neg_a", [P, NH])
        alpha = a.sb("alpha", [P, NT * NH])
        alpha_rows = a.sb("alpha_rows", [P, 2, P])
        logits = a.bank("logits")
        turned = a.bank("turned")
        loaded, projected = a.sem("loaded"), a.sem("projected")
        beta_read, y_made = a.sem("beta_read"), a.sem("y_made")
        exp_made, ln_made, expa_made = a.sem("exp_made"), a.sem("ln_made"), a.sem("expa_made")
        step, arg_made, alpha_made = a.sem("step"), a.sem("arg_made"), a.sem("alpha_made")
        alpha_turned, rows_made, stored = a.sem("alpha_turned"), a.sem("rows_made"), a.sem("stored")
        proj = logits[:, :].rearrange("p (t n) -> p t n", t=NT)
        with nc.Block() as block:

            @block.sync
            def _(sp):
                sp.dma_start(w[:], w_ba).then_inc(loaded, 16)
                sp.dma_start(la[:], log_a).then_inc(loaded, 16)
                sp.dma_start(dt[:], dt_bias).then_inc(loaded, 16)
                sp.wait_ge(rows_made, 1)
                sp.dma_start(alpha_dram.rearrange("(a p) m -> p a m", a=2), alpha_rows[:]).then_inc(stored, 16)
                sp.wait_ge(stored, 16)

            @block.tensor
            def _(pe):
                pe.wait_ge(loaded, 48)
                for t in range(NT):
                    for k in range(KC):
                        mm = pe.matmul(proj[:, t, :], x_t[:, k, t * P:(t + 1) * P], w[:, k, :],
                                       start=(k == 0), stop=(k == KC - 1))
                mm.then_inc(projected, 1)
                pe.wait_ge(alpha_made, 1)
                for n in range(2):
                    mm = pe.transpose(turned[:, n * P:(n + 1) * P], alpha[:, n * P:(n + 1) * P], ident)
                mm.then_inc(alpha_turned, 1)

            @block.scalar
            def _(act):
                act.wait_ge(projected, 1)
                for j in range(VH):
                    for c in range(NC):
                        op = act.activation(
                            beta_cols.rearrange("p (g b j c) -> p b g j c", g=GH, b=B, j=VH)[:, :, :, j, c],
                            proj[:, :, 0:NH].rearrange("p (b c) (g j) -> p b c g j", c=NC, j=VH)[:, :, c, :, j],
                            ACT.Sigmoid)
                op.then_inc(beta_read, 1)
                act.wait_ge(y_made, 1)
                act.activation(u[:], w1[:], ACT.Exp, scale=-1.0).then_inc(exp_made, 1)
                act.activation(neg_a[:], la[:], ACT.Exp).then_inc(expa_made, 1)
                act.wait_ge(exp_made, 1)
                act.activation(small[:], u[:], ACT.Ln, bias=1.0).then_inc(ln_made, 1)
                act.wait_ge(arg_made, 1)
                act.activation(alpha[:], big[:], ACT.Exp, scale=-1.0).then_inc(alpha_made, 1)

            @block.vector
            def _(v):
                n = 0

                def then(op):
                    nonlocal n
                    n += 1
                    op.then_inc(step, 1)
                    v.wait_ge(step, n)

                v.wait_ge(beta_read, 1)
                y5 = y[:].rearrange("p (g b j c) -> p g b j c", g=GH, b=B, j=VH)
                for j in range(VH):
                    for c in range(NC):
                        op = v.tensor_tensor(
                            y5[:, :, :, j, c],
                            proj[:, :, NH:].rearrange("p (b c) (g j) -> p g b c j", c=NC, j=VH)[:, :, :, c, j],
                            dt[:].rearrange("p (g j) -> p g j", j=VH)[:, :, j:j + 1].to_broadcast([P, GH, B]),
                            ALU.add)
                then(op)
                then(v.tensor_scalar(big[:], y[:], 0.0, None, ALU.max))
                then(v.tensor_scalar(w1[:], y[:], 0.0, -1.0, ALU.min, ALU.mult))
                v.tensor_tensor(w1[:], w1[:], big[:], ALU.add).then_inc(y_made, 1)
                v.wait_ge(exp_made, 1)
                then(v.tensor_scalar(poly[:], u[:], 1.0 / 7, -1.0 / 6, ALU.mult, ALU.add))
                for c in (1.0 / 5, -1.0 / 4, 1.0 / 3, -1.0 / 2, 1.0):
                    then(v.tensor_tensor(poly[:], poly[:], u[:], ALU.mult))
                    then(v.tensor_scalar(poly[:], poly[:], c, None, ALU.add))
                then(v.tensor_tensor(poly[:], poly[:], u[:], ALU.mult))
                then(v.tensor_scalar(w1[:], u[:], 0.1, None, ALU.is_lt))
                v.wait_ge(ln_made, 1)
                then(v.tensor_tensor(poly[:], poly[:], small[:], ALU.subtract))
                then(v.tensor_tensor(poly[:], poly[:], w1[:], ALU.mult))
                then(v.tensor_tensor(poly[:], poly[:], small[:], ALU.add))
                then(v.tensor_tensor(poly[:], poly[:], big[:], ALU.add))
                v.wait_ge(expa_made, 1)
                for j in range(VH):
                    op = v.tensor_tensor(
                        big[:].rearrange("p (g b j c) -> p g b j c", g=GH, b=B, j=VH)[:, :, :, j, :],
                        poly[:].rearrange("p (g b j c) -> p g b j c", g=GH, b=B, j=VH)[:, :, :, j, :],
                        neg_a[:].rearrange("p (g j o) -> p g j o", j=VH, o=1)[:, :, j:j + 1, :]
                        .to_broadcast([P, GH, B, NC]),
                        ALU.mult)
                op.then_inc(arg_made, 1)
                v.wait_ge(alpha_turned, 1)
                v.tensor_copy(alpha_rows[:], turned[:, 0:2 * P].rearrange("p (a m) -> p a m", a=2)).then_inc(rows_made, 1)
        a.clear()


def delta_phase(nc, tokens, x_t, w_in, conv_w, w_out, rms_w, ident, masks, beta_cols, alpha_dram):
    neg_first, joins = masks
    with ExitStack() as stack:
        a = Space(nc, stack, "dr_")
        w_g = a.sb("w_g", [P, KC, 6 * P])
        taps = a.sb("taps", [P, 4, TAPS])
        wo_g = a.sb("wo_g", [P, VH, D])
        rms = a.sb("rms", [P, 1])
        zeros = a.sb("zeros", [P, P])
        ones = a.sb("ones", [P, P])
        eps_q = a.sb("eps_q", [P, 1])
        eps_k = a.sb("eps_k", [P, 1])
        alpha = a.sb("alpha", [P, 2, VH, S])
        beta = a.sb("beta", [P, 2, VH, NC])
        conv_qk = a.sb("conv_qk", [P, 2, S])
        conv_v = a.sb("conv_v", [P, VH, S])
        qk_act = a.sb("qk_act", [P, 2 * S])
        qk_sq = a.sb("qk_sq", [P, 2 * S])
        norms = a.sb("norms", [P, 2 * S])
        qk = a.sb("qk", [P, 2, 2, S])
        v_t = a.sb("v_t", [P, VH, S])
        gate = a.sb("gate", [P, 2, VH * S])
        decay = a.sb("decay", [P, 2, VH, NC, P])
        p_row = a.sb("p_row", [P, 2, VH, P])
        kq_p = a.sb("kq_p", [P, 2, VH, 2, P])
        n_mat = a.sb("n_mat", [P, VH, NC, P])
        qk_dec = a.sb("qk_dec", [P, 2, VH, NC, P])
        yx = a.sb("yx", [P, 2, VH, 2, NC, P])
        first = a.sb("first", [P, VH, NC, P])
        f_mask = a.sb("f_mask", [P, VH, NC, P])
        k_tok = a.sb("k_tok", [P, 2, P])
        v_tok = a.sb("v_tok", [P, 2, VH, NC, P])
        u0 = a.sb("u0", [P, VH, P])
        u0d = a.sb("u0d", [P, VH, P])
        state = a.sb("state", [P, VH, P])
        r1 = a.sb("r1", [P, VH, P])
        u1 = a.sb("u1", [P, VH, P])
        squares = a.sb("squares", [P, VH * NC, P])
        sumsq = a.sb("sumsq", [P, VH * NC])
        rms_den = a.sb("rms_den", [P, VH * NC])
        rms_inv = a.sb("rms_inv", [P, VH * NC])
        o_norm = a.sb("o_norm", [P, VH * NC, P])
        gated = a.sb("gated", [P, VH, S])

        bank_a, bank_b = a.bank("a"), a.bank("b")
        bank_f = [a.bank(f"f{j}") for j in range(VH)]
        bank_g = [a.bank(f"g{j}") for j in range(VH)]
        bank_m, bank_n = a.bank("m"), a.bank("n")

        sem = a.sem
        consts, consts_made = sem("consts"), sem("consts_made")
        weights_loaded, w_out_loaded = sem("weights_loaded"), sem("w_out_loaded")
        alpha_loaded = [sem(f"alpha_loaded{par}") for par in range(2)]
        qk_projected, v_projected, gate_projected = sem("qk_projected"), sem("v_projected"), sem("gate_projected")
        qk_tapped, v_tapped, conv_step = sem("qk_tapped"), sem("v_tapped"), sem("conv_step")
        qk_activated, qk_squared, qk_summed = sem("qk_activated"), sem("qk_squared"), sem("qk_summed")
        norms_made, norms_inverted, qk_ready = sem("norms_made"), sem("norms_inverted"), sem("qk_ready")
        v_ready, gate_ready = sem("v_ready"), sem("gate_ready")
        decay_made, beta_copied = sem("decay_made"), sem("beta_copied")
        kq_done, turned, tok_copied = sem("kq_done"), sem("turned"), sem("tok_copied")
        n_made, kq_p_made = sem("n_made"), sem("kq_p_made")
        first_masked, y_started, x_turned, x_started = sem("first_masked"), sem("y_started"), sem("x_turned"), sem("x_started")
        f_done = [sem(f"f_done{j}") for j in range(VH)]
        f_masked = [sem(f"f_masked{j}") for j in range(VH)]
        g_done = [sem(f"g_done{j}") for j in range(VH)]
        yx_done = [sem(f"yx_done{j}") for j in range(VH)]
        w0_done, u0_made, u0d_made = sem("w0_done"), sem("u0_made"), sem("u0d_made")
        s_done, s_copied, ks_done, r1_made = sem("s_done"), sem("s_copied"), sem("ks_done"), sem("r1_made")
        w1_done, u1_made, o_done = sem("w1_done"), sem("u1_made"), sem("o_done")
        o_squared, rms_rooted, rms_inverted, o_normed = sem("o_squared"), sem("rms_rooted"), sem("rms_inverted"), sem("o_normed")
        o_turned, gated_made, y_done, y_added = sem("o_turned"), sem("gated_made"), sem("y_done"), sem("y_added")

        JOINS = LEVELS - 1

        def pe_project(pe, out, m, wanted):
            for k in range(KC):
                mm = pe.matmul(out, w_g[:, k, m * P:(m + 1) * P], x_t[:, k, bass.ds(wanted * S, S)],
                               start=(k == 0), stop=(k == KC - 1))
            return mm

        def pe_slot(pe, u, par, project, solve, post):
            oth = 1 - par
            b_next = (u + 1) % B

            def f_step(s, j):
                if s == 1:
                    wait(pe, x_started, u + 1)
                    wait(pe, y_started, u + 1)
                else:
                    wait(pe, yx_done[j], JOINS * u + s - 1)
                for c in range(NC):
                    mm = pe.matmul(bank_f[j][:, c * P:(c + 1) * P], n_mat[:, j, c, :], yx[:, par, j, 1, c, :],
                                   start=True, stop=True)
                mm.then_inc(f_done[j], 1)

            def g_step(s, j):
                wait(pe, f_masked[j], JOINS * u + s)
                for c in range(NC):
                    mm = pe.matmul(bank_g[j][:, c * P:(c + 1) * P], f_mask[:, j, c, :], yx[:, par, j, 0, c, :],
                                   start=True, stop=True)
                    if s < JOINS:
                        mm = pe.matmul(bank_g[j][:, (NC + c) * P:(NC + c + 1) * P], yx[:, par, j, 0, c, :],
                                       f_mask[:, j, c, :], start=True, stop=True)
                mm.then_inc(g_done[j], 1)

            if solve:
                wait(pe, qk_ready, u + 1)
                wait(pe, y_added, 2 * (u - 1))
                for c in range(NC):
                    mm = pe.matmul(bank_m[:, c * 2 * P:(c + 1) * 2 * P], qk[:, par, 1, c * P:(c + 1) * P],
                                   qk[:, par, :, c * P:(c + 1) * P], start=True, stop=True)
                mm.then_inc(kq_done, 1)
                wait(pe, v_ready, u + 1)
                for j in range(VH):
                    for c in range(NC):
                        pe.transpose(bank_n[:, (j * NC + c) * P:(j * NC + c + 1) * P],
                                     v_t[:, j, c * P:(c + 1) * P], ident)
                pe.transpose(bank_f[0][:, 0:P], qk[:, par, 1, 0:P], ident).then_inc(turned, 1)
            if project:
                wait(pe, alpha_loaded[oth], 16 * ((u + 3) // 2))
                wait(pe, gate_ready, u + 1)
                pe_project(pe, bank_a[:, 0:S], 0, b_next)
                pe_project(pe, bank_a[:, S:2 * S], 1, b_next).then_inc(qk_projected, 1)
            if solve:
                wait(pe, y_started, u + 1)
                wait(pe, tok_copied, u + 1)
                for j in range(VH):
                    wait(pe, yx_done[j], JOINS * u)
                    for c in range(NC):
                        mm = pe.transpose(bank_g[j][:, c * P:(c + 1) * P], yx[:, par, j, 0, c, :], ident)
                mm.then_inc(x_turned, 1)
            if post:
                if solve:
                    wait(pe, n_made, u + 1)
                else:
                    wait(pe, y_added, 2 * (u - 1))
                for j in range(VH):
                    wait(pe, yx_done[j], JOINS * u)
                    mm = pe.matmul(bank_m[:, j * P:(j + 1) * P], yx[:, oth, j, 0, 0, :], v_tok[:, oth, j, 0, :],
                                   start=True, stop=True)
                mm.then_inc(w0_done, 1)

            def post_state():
                wait(pe, u0d_made, u)
                for j in range(VH):
                    mm = pe.matmul(bank_n[:, j * P:(j + 1) * P], k_tok[:, oth, :], u0d[:, j, :], start=True, stop=True)
                mm.then_inc(s_done, 1)

            def post_carry():
                wait(pe, s_copied, u)
                wait(pe, kq_p_made, u)
                for j in range(VH):
                    mm = pe.matmul(bank_m[:, j * P:(j + 1) * P], kq_p[:, oth, j, 1, :], state[:, j, :],
                                   start=True, stop=True)
                mm.then_inc(ks_done, 1)

            def post_w1():
                wait(pe, r1_made, u)
                for j in range(VH):
                    mm = pe.matmul(bank_n[:, j * P:(j + 1) * P], yx[:, oth, j, 0, 1, :], r1[:, j, :],
                                   start=True, stop=True)
                mm.then_inc(w1_done, 1)

            def post_o():
                wait(pe, u1_made, u)
                for j in range(VH):
                    at = j * NC * P
                    pe.matmul(bank_m[:, at:at + P], qk_dec[:, oth, j, 0, :], u0[:, j, :], start=True, stop=True)
                    pe.matmul(bank_m[:, at + P:at + 2 * P], qk_dec[:, oth, j, 1, :], u1[:, j, :],
                              start=True, stop=False)
                    mm = pe.matmul(bank_m[:, at + P:at + 2 * P], kq_p[:, oth, j, 0, :], state[:, j, :],
                                   start=False, stop=True)
                mm.then_inc(o_done, 1)

            def post_turn():
                wait(pe, o_normed, u)
                for n in range(VH * NC):
                    mm = pe.transpose(bank_n[:, n * P:(n + 1) * P], o_norm[:, n, :], ident)
                mm.then_inc(o_turned, 1)

            def post_out():
                wait(pe, gated_made, u)
                wait(pe, w_out_loaded, 16 * ((u - 1) // B + 1))
                for c, bank in enumerate((bank_m, bank_n)):
                    for j in range(VH):
                        mm = pe.matmul(bank[:, :], gated[:, j, c * P:(c + 1) * P], wo_g[:, j, :],
                                       start=(j == 0), stop=(j == VH - 1))
                    mm.then_inc(y_done, 1)

            def v_part(j):
                mm = pe_project(pe, bank_b[:, j * S:(j + 1) * S], 2 + j, b_next)
                if j == VH - 1:
                    mm.then_inc(v_projected, 1)

            def g_part(j):
                if j == 0:
                    wait(pe, conv_step, 12 * (u + 1) + 6)
                mm = pe_project(pe, bank_a[:, j * S:(j + 1) * S], 4 + j, b_next)
                if j == VH - 1:
                    mm.then_inc(gate_projected, 1)

            def sum_part():
                wait(pe, qk_squared, u + 2)
                wait(pe, conv_step, 12 * (u + 2))
                pe.matmul(bank_b[:, :], ones[:, :], qk_sq[:, :], start=True, stop=True).then_inc(qk_summed, 1)

            if project:
                wait(pe, norms_made, u + 1)
            fills = {(1, 0): [(project, lambda: v_part(0))], (1, 1): [(post, post_state)],
                     (2, 0): [(project, lambda: v_part(1))], (2, 1): [(post, post_carry)],
                     (3, 0): [(project, lambda: g_part(0))], (3, 1): [(post, post_w1)],
                     (4, 0): [(project, sum_part)], (4, 1): [(post, post_o)],
                     (6, 0): [(post, post_turn)],
                     (6, 1): [(project, lambda: g_part(1)), (post, post_out)]}
            for s in range(1, LEVELS):
                for half in range(2):
                    if solve:
                        for j in range(VH):
                            (f_step, g_step)[half](s, j)
                    for wanted, part in fills.get((s, half), []):
                        if wanted:
                            part()

        def act_slot(act, u, par, project, solve, post):
            oth = 1 - par
            if solve:
                wait(act, turned, u + 1)
                act.activation(k_tok[:, par, :], bank_f[0][:, 0:P], ACT.Copy)
                act.activation(v_tok[:, par].rearrange("p j c n -> p (j c n)"), bank_n[:, :], ACT.Copy)\
                    .then_inc(tok_copied, 1)
            if project:
                wait(act, qk_projected, u + 2)
                for m in range(2):
                    op = act.activation(conv_qk[:, m, :], bank_a[:, m * S:(m + 1) * S], ACT.Copy,
                                        scale=taps[:, m, TAPS - 1:TAPS])
                op.then_inc(qk_tapped, 1)
            if solve:
                wait(act, x_turned, u + 1)
                for j in range(VH):
                    op = act.activation(yx[:, par, j, 1].rearrange("p c n -> p (c n)"), bank_g[j][:, 0:NC * P], ACT.Copy)
                op.then_inc(x_started, 1)
            if post:
                wait(act, w0_done, u)
                for j in range(VH):
                    op = act.activation(u0[:, j, :], bank_m[:, j * P:(j + 1) * P], ACT.Copy, scale=beta[:, oth, j, 0:1])
                op.then_inc(u0_made, 1)
            if project:
                wait(act, conv_step, 12 * (u + 1) + 6)
                act.activation(qk_act[:, :], conv_qk[:].rearrange("p m n -> p (m n)"), ACT.Silu).then_inc(qk_activated, 1)
                wait(act, qk_activated, u + 2)
                act.activation(qk_sq[:, :], qk_act[:, :], ACT.Square).then_inc(qk_squared, 1)
            if post:
                wait(act, s_done, u)
                act.activation(state[:].rearrange("p j n -> p (j n)"), bank_n[:, 0:VH * P], ACT.Copy).then_inc(s_copied, 1)
            if project:
                wait(act, v_projected, u + 2)
                for j in range(VH):
                    op = act.activation(conv_v[:, j, :], bank_b[:, j * S:(j + 1) * S], ACT.Copy,
                                        scale=taps[:, 2 + j, TAPS - 1:TAPS])
                op.then_inc(v_tapped, 1)
            if post:
                wait(act, w1_done, u)
                for j in range(VH):
                    op = act.activation(u1[:, j, :], bank_n[:, j * P:(j + 1) * P], ACT.Copy, scale=beta[:, oth, j, 1:2])
                op.then_inc(u1_made, 1)
            if project:
                wait(act, conv_step, 12 * (u + 2))
                act.activation(v_t[:].rearrange("p j n -> p (j n)"), conv_v[:].rearrange("p j n -> p (j n)"), ACT.Silu)\
                    .then_inc(v_ready, 1)
                wait(act, qk_summed, u + 2)
                act.activation(norms[:, 0:S], bank_b[:, 0:S], ACT.Sqrt, scale=float(P), bias=eps_q[:, 0:1])
                act.activation(norms[:, S:2 * S], bank_b[:, S:2 * S], ACT.Sqrt, bias=eps_k[:, 0:1]).then_inc(norms_made, 1)
            if post:
                wait(act, o_done, u)
                wait(act, o_squared, u - 1)
                for n in range(VH * NC):
                    op = act.activation(squares[:, n, :], bank_m[:, n * P:(n + 1) * P], ACT.Square,
                                        accum_out=sumsq[:, n:n + 1])
                op.then_inc(o_squared, 1)
                wait(act, o_squared, u)
                act.activation(rms_den[:, :], sumsq[:, :], ACT.Sqrt, scale=1.0 / P, bias=eps_k[:, 0:1]).then_inc(rms_rooted, 1)
            if project:
                wait(act, gate_projected, u + 2)
                if post:
                    wait(act, gated_made, u)
                act.activation(gate[:, oth, :], bank_a[:, :], ACT.Silu).then_inc(gate_ready, 1)

        def conv(v, u, acc, bank, m0, base):
            n = base
            for d in range(1, TAPS):
                for m in range(2):
                    if d > 1:
                        wait(v, conv_step, n - 1)
                    v.scalar_tensor_tensor(out=acc[:, m, d:S], in0=bank[:, m * S:(m + 1) * S - d],
                                           scalar=taps[:, m0 + m, TAPS - 1 - d:TAPS - d], in1=acc[:, m, d:S],
                                           op0=ALU.mult, op1=ALU.add).then_inc(conv_step, 1)
                    n = n + 1

        def dve_slot(v, u, par, project, solve, post):
            oth = 1 - par
            if solve:
                wait(v, kq_done, u + 1)
                wait(v, decay_made, u + 1)
                wait(v, beta_copied, u + 1)
                products = bank_m[:].rearrange("p (c m n) -> p m c n", c=NC, m=2)
                for j in range(VH):
                    for c in range(NC):
                        v.scalar_tensor_tensor(out=n_mat[:, j, c, :], in0=products[:, 1, c, :], scalar=beta[:, par, j, c:c + 1],
                                               in1=decay[:, par, j, c, :], op0=ALU.mult, op1=ALU.mult)
                for j in range(VH):
                    op = v.tensor_tensor(qk_dec[:, par, j], products[:, 0], decay[:, par, j], ALU.mult)
                op.then_inc(n_made, 1)
                for j in range(VH):
                    op = v.tensor_tensor(kq_p[:, par, j], qk[:, par, :, P:2 * P],
                                         p_row[:, par, j:j + 1, :].to_broadcast([P, 2, P]), ALU.mult)
                op.then_inc(kq_p_made, 1)
            if project:
                wait(v, qk_tapped, u + 2)
                conv(v, u, conv_qk, bank_a, 0, 12 * (u + 1))

            def fill_v():
                wait(v, v_tapped, u + 2)
                conv(v, u, conv_v, bank_b, 2, 12 * (u + 1) + 6)

            def fill_r1():
                wait(v, ks_done, u)
                v.tensor_tensor(r1[:], v_tok[:, oth, :, 1, :], bank_m[:, 0:VH * P].rearrange("p (j n) -> p j n", j=VH),
                                ALU.subtract).then_inc(r1_made, 1)

            def fill_norm(m):
                if m == 0:
                    wait(v, norms_made, u + 2)
                v.reciprocal(norms[:, m * S:(m + 1) * S], norms[:, m * S:(m + 1) * S]).then_inc(norms_inverted, 1)
                if m == 0:
                    return
                wait(v, norms_inverted, 2 * (u + 2))
                v.tensor_tensor(qk[:, oth].rearrange("p m n -> p (m n)"), qk_act[:, :], norms[:, :], ALU.mult)\
                    .then_inc(qk_ready, 1)

            def fill_o():
                wait(v, rms_rooted, u)
                v.reciprocal(rms_inv[:, :], rms_den[:, :]).then_inc(rms_inverted, 1)
                wait(v, rms_inverted, u)
                v.tensor_tensor(o_norm[:], bank_m[:].rearrange("p (n m) -> p n m", n=VH * NC),
                                rms_inv[:, :, None].to_broadcast([P, VH * NC, P]), ALU.mult).then_inc(o_normed, 1)

            def fill_gated():
                wait(v, o_turned, u)
                wait(v, gate_ready, u)
                v.scalar_tensor_tensor(out=gated[:].rearrange("p j n -> p (j n)"), in0=bank_n[:, :], scalar=rms[:, 0:1],
                                       in1=gate[:, oth, :], op0=ALU.mult, op1=ALU.mult).then_inc(gated_made, 1)

            def fill_decay():
                wait(v, alpha_loaded[oth], 16 * ((u + 3) // 2))
                if post:
                    wait(v, u0d_made, u)
                for j in range(VH):
                    for c in range(NC):
                        v.tensor_tensor_scan(decay[:, oth, j, c, :], alpha[:, oth, j, c * P:(c + 1) * P], ident, 0.0,
                                             ALU.mult, ALU.add)
                    op = v.tensor_tensor_scan(p_row[:, oth, j, :], alpha[:, oth, j, P:2 * P], zeros[:, :], 1.0,
                                              ALU.mult, ALU.add)
                op.then_inc(decay_made, 1)

            def fill_add():
                b_prev = (u - 1) % B
                for c, bank in enumerate((bank_m, bank_n)):
                    wait(v, y_done, 2 * (u - 1) + c + 1)
                    at = tokens[:, bass.ds(b_prev * NC + c, 1), :]
                    v.tensor_tensor(at, at, bank[:].rearrange("p (o n) -> p o n", o=1), ALU.add).then_inc(y_added, 1)

            fills = {2: [(project, fill_v)], 3: [(post, fill_r1)], 4: [(project, lambda: fill_norm(0))],
                     5: [(post, fill_o)], 6: [(project, lambda: fill_norm(1))]}
            for s in range(1, LEVELS):
                if solve:
                    for j in range(VH):
                        wait(v, f_done[j], JOINS * u + s)
                        v.tensor_tensor(f_mask[:, j], bank_f[j][:, 0:NC * P].rearrange("p (c n) -> p c n", c=NC),
                                        joins[:, s - 1:s, :].to_broadcast([P, NC, P]), ALU.mult).then_inc(f_masked[j], 1)
                    if s == JOINS and post:
                        fill_gated()
                    for j in range(VH):
                        wait(v, g_done[j], JOINS * u + s)
                        w = 2 * NC * P if s < JOINS else NC * P
                        at = yx[:, par, j].rearrange("p m c n -> p (m c n)")[:, 0:w]
                        v.tensor_tensor(at, at, bank_g[j][:, 0:w], ALU.subtract).then_inc(yx_done[j], 1)
                elif s == JOINS and post:
                    fill_gated()
                for wanted, part in fills.get(s, []):
                    if wanted:
                        part()
            if project:
                fill_decay()
            if post:
                fill_add()

        def pool_slot(g, u, par, project, solve, post):
            oth = 1 - par
            if solve:
                wait(g, n_made, u + 1)
                for j in range(VH):
                    op = g.tensor_tensor(first[:, j], n_mat[:, j], neg_first, ALU.mult)
                op.then_inc(first_masked, 1)
                wait(g, first_masked, u + 1)
                for j in range(VH):
                    op = g.tensor_tensor(yx[:, par, j, 0], first[:, j],
                                         ident[:, None, :].to_broadcast([P, NC, P]), ALU.add)
                op.then_inc(y_started, 1)
            if post:
                wait(g, u0_made, u)
                g.tensor_tensor(u0d[:], u0[:], decay[:, oth, :, 0, P - 1:P].to_broadcast([P, VH, P]), ALU.mult)\
                    .then_inc(u0d_made, 1)
            if project:
                if post:
                    wait(g, u1_made, u)
                g.tensor_copy(beta[:, oth].rearrange("p j c -> p (j c)"),
                              beta_cols[:, bass.ds((u + 1) * VH * NC, VH * NC)]).then_inc(beta_copied, 1)

        def slots(engine, slot):
            slot(engine, -1, 1, True, False, False)
            slot(engine, 0, 0, True, True, False)
            slot(engine, 1, 1, True, True, True)
            slot(engine, 2, 0, True, True, True)
            with engine.Fori(1, (UNITS - 2) // 2) as i:
                slot(engine, 2 * i + 1, 1, True, True, True)
                slot(engine, 2 * i + 2, 0, True, True, True)
            slot(engine, UNITS - 1, 1, False, True, True)
            slot(engine, UNITS, 0, False, False, True)

        with nc.Block() as block:

            @block.sync
            def _(sp):
                sp.dma_start(rms[:], rms_w).then_inc(consts, 16)
                sp.wait_ge(consts_made, 1)

                def rows(u, par, before):
                    wait(sp, decay_made, before)
                    sp.dma_start(alpha[:, par], alpha_dram[bass.ds(u, 1), :].rearrange("o n -> (o n)")
                                 .partition_broadcast(P).rearrange("p (j n) -> p j n", j=VH)).then_inc(alpha_loaded[par], 16)

                def group(g, first_group):
                    wait(sp, gate_projected, B * g)
                    wait(sp, v_ready, B * g)
                    sp.dma_start(w_g[:], w_in[bass.ds(g, 1)].rearrange("o p k n -> (o p) k n")).then_inc(weights_loaded, 16)
                    sp.dma_start(taps[:], conv_w[bass.ds(g, 1)].rearrange("o p m n -> (o p) m n")).then_inc(weights_loaded, 16)
                    wait(sp, weights_loaded, 32 * (g + 1))
                    if first_group:
                        wait(sp, consts, 16)
                    rows(B * g, 0, B * g)
                    rows(B * g + 1, 1, B * g)
                    wait(sp, y_done, 2 * B * g)
                    sp.dma_start(wo_g[:], w_out[bass.ds(g, 1)].rearrange("o p j n -> (o p) j n")).then_inc(w_out_loaded, 16)
                    for b in range(2, B):
                        rows(B * g + b, b % 2, B * g + b - 1)

                group(0, True)
                with sp.Fori(1, GH) as g:
                    group(g, False)

            @block.tensor
            def _(pe):
                pe.wait_ge(consts_made, 1)
                slots(pe, pe_slot)

            @block.scalar
            def _(act):
                act.wait_ge(consts_made, 1)
                slots(act, act_slot)

            @block.vector
            def _(v):
                v.memset(eps_q[:], P * DELTA_EPS)
                v.memset(eps_k[:], DELTA_EPS)
                v.memset(ones[:], 1.0)
                v.memset(zeros[:], 0.0).then_inc(consts_made, 1)
                v.wait_ge(consts_made, 1)
                slots(v, dve_slot)
                v.wait_ge(y_added, 2 * UNITS)

            @block.gpsimd
            def _(g):
                slots(g, pool_slot)
        a.clear()


def load_phase(nc, loads):
    with ExitStack() as stack:
        a = Space(nc, stack, "ld_")
        loaded = a.sem("loaded")
        with nc.Block() as block:

            @block.sync
            def _(sp):
                for to, source in loads:
                    sp.dma_start(to, source).then_inc(loaded, 16)
                sp.wait_ge(loaded, 16 * len(loads))
        a.clear()


def norm_phase(nc, name, tokens, ident=None, turned=None, out=None):
    with ExitStack() as stack:
        a = Space(nc, stack, name + "_")
        stats = a.sb("stats", [P, NT, 6])
        moments = a.sb("moments", [P, NT, 2])
        den = a.sb("den", [P, NT])
        eps = a.sb("eps", [P, 1])
        banks = [a.bank(f"turn{n}") for n in range(4)]
        eps_made, stats_made, moments_made = a.sem("eps_made"), a.sem("stats_made"), a.sem("moments_made")
        rooted, inverted, normed = a.sem("rooted"), a.sem("inverted"), a.sem("normed")
        stored, transposed, copied = a.sem("stored"), a.sem("transposed"), a.sem("copied")
        with nc.Block() as block:

            @block.vector
            def _(v):
                v.memset(eps[:], LN_EPS).then_inc(eps_made, 1)
                for t in range(NT):
                    op = v.bn_stats(stats[:, t, :], tokens[:, t, :])
                op.then_inc(stats_made, 1)
                v.wait_ge(stats_made, 1)
                for t in range(NT):
                    op = v.bn_aggr(moments[:, t, :], stats[:, t, :])
                op.then_inc(moments_made, 1)
                v.wait_ge(rooted, 1)
                v.reciprocal(den[:, :], den[:, :]).then_inc(inverted, 1)
                v.wait_ge(inverted, 1)
                for t in range(NT):
                    v.tensor_scalar(tokens[:, t, :], tokens[:, t, :], moments[:, t, 0:1], den[:, t:t + 1],
                                    ALU.subtract, ALU.mult).then_inc(normed, 1)

            @block.tensor
            def _(pe):
                if turned is not None:
                    for t in range(NT):
                        pe.wait_ge(normed, t + 1)
                        wait(pe, copied, t - len(banks) + 1)
                        for k in range(KC):
                            mm = pe.transpose(banks[t % 4][:, k * P:(k + 1) * P], tokens[:, t, k * P:(k + 1) * P], ident)
                        mm.then_inc(transposed, 1)

            @block.scalar
            def _(act):
                act.wait_ge(eps_made, 1)
                act.wait_ge(moments_made, 1)
                act.activation(den[:, :], moments[:, :, 1], ACT.Sqrt, bias=eps[:, 0:1]).then_inc(rooted, 1)
                if turned is not None:
                    for t in range(NT):
                        act.wait_ge(transposed, t + 1)
                        act.activation(turned[:, :, t * P:(t + 1) * P],
                                       banks[t % 4][:].rearrange("p (k n) -> p k n", k=KC), ACT.Copy).then_inc(copied, 1)

            @block.sync
            def _(sp):
                if out is not None:
                    for t in range(NT):
                        sp.wait_ge(normed, t + 1)
                        sp.dma_start(out[t], tokens[:, t, :]).then_inc(stored, 16)
                    sp.wait_ge(stored, 16 * NT)


XH, XD = 32, 16
XT = D // P
PAIRS = XH // 2
QT = S // P
KT = S // P


def cross_phase(nc, tokens, x_t, ctx_dram, mask_dram, weights, tanh_gate_src, tables, ident):
    w_q_dram, w_k_dram, w_v_dram, w_o_dram = weights
    cos_dram, sin_dram, turn_dram, halves_dram = tables
    with ExitStack() as stack:
        a = Space(nc, stack, "xa_")
        w_q, w_k, w_v, w_o = (a.sb(n, [P, KC, D]) for n in ("w_q", "w_k", "w_v", "w_o"))
        cos, sin = a.sb("cos", [P, S]), a.sb("sin", [P, S])
        turn = a.sb("turn", [P, P])
        halves = a.sb("halves", [P, 2])
        gate_in = a.sb("gate_in", [P, XH])
        gains = a.sb("gains", [P, PAIRS, 2, 2])
        x_b = a.sb("x_b", [P, KC, S])
        ctx_b = a.sb("ctx_b", [P, KC, S])
        mask = a.sb("mask", [P, QT, S])
        mask_in = a.sb("mask_in", [P, QT, S])
        q_raw = a.sb("q_raw", [P, XT, S])
        k_raw = a.sb("k_raw", [P, XT, S])
        q_rot = a.sb("q_rot", [P, XT, S])
        k_rot = a.sb("k_rot", [P, XT, S])
        k_pair = a.sb("k_pair", [P, XT, 2, S])
        ak_pair = a.sb("ak_pair", [P, XT, 2, S])
        val = a.sb("val", [P, 2, KT, D])
        scores = a.sb("scores", [P, 2, 2, S])
        top = a.sb("top", [P, 2, 2, 2])
        probs = a.sb("probs", [P, 2, 3, 2, S])
        probs_t = a.sb("probs_t", [P, 2, 2, 2, KT, P])
        sums = a.sb("sums", [P, 2, 2, 2])
        shares = a.sb("shares", [P, 2, 2, 2])
        second = a.sb("second", [P, P])
        attn_t = a.sb("attn_t", [P, XT, S])

        bank_s = [[a.bank(f"s{k}{n}") for n in range(2)] for k in range(2)]
        bank_t = [a.bank(f"t{k}") for k in range(2)]
        bank_o = [a.bank(f"o{k}") for k in range(2)]

        sem = a.sem
        consts, gains_set, gate_made = sem("consts"), sem("gains_set"), sem("gate_made")
        x_copied, ctx_loaded, mask_loaded, mask_guarded = sem("x_copied"), sem("ctx_loaded"), sem("mask_loaded"), sem("mask_guarded")
        q_projected, k_projected, ak_projected = sem("q_projected"), sem("k_projected"), sem("ak_projected")
        q_copied, k_copied, ak_copied = sem("q_copied"), sem("k_copied"), sem("ak_copied")
        q_turned, k_turned, step = sem("q_turned"), sem("k_turned"), sem("step")
        q_ready, k_rotated, k_ready = sem("q_ready"), sem("k_rotated"), sem("k_ready")
        v_projected, v_copied, av_projected, av_copied = sem("v_projected"), sem("v_copied"), sem("av_projected"), sem("av_copied")
        scored = [sem(f"scored{k}") for k in range(2)]
        masked = sem("masked")
        topped = [sem(f"topped{k}") for k in range(2)]
        exped = [sem(f"exped{k}") for k in range(2)]
        p_turned = [sem(f"p_turned{k}") for k in range(2)]
        p_copied = [sem(f"p_copied{k}") for k in range(2)]
        shared, gained = sem("shared"), sem("gained")
        scaled = [sem(f"scaled{k}") for k in range(2)]
        group_done, second_taken, extracted = sem("group_done"), sem("second_taken"), sem("extracted")
        y_done, y_added = sem("y_done"), sem("y_added")

        N = QT * PAIRS
        GROUPS = N // 4

        def row(n):
            return n // PAIRS, n % PAIRS // 4, 32 * (n % 4)

        def pe_batch(pe, b):
            def project(bank, w, m, src):
                for h in range(2):
                    for k in range(KC):
                        mm = pe.matmul(bank[:, h * S:(h + 1) * S], w[:, k, (m + h) * P:(m + h + 1) * P], src[:, k, :],
                                       start=(k == 0), stop=(k == KC - 1))
                return mm

            def values(bank, t, src):
                for k in range(KC):
                    mm = pe.matmul(bank[:, :], src[:, k, t * P:(t + 1) * P], w_v[:, k, :], start=(k == 0), stop=(k == KC - 1))
                return mm

            def score(n):
                q, t, r = row(n)
                for kind, keys in enumerate((k_pair, ak_pair)):
                    if n >= 2:
                        wait(pe, masked if kind == 0 else exped[1], N * b + n - 1)
                    pe.matmul(bank_s[kind][n % 2][:, :], q_rot[r:r + 32, t, q * P:(q + 1) * P],
                              keys[r:r + 32, t].rearrange("p h n -> p (h n)"), start=True, stop=True)\
                        .then_inc(scored[kind], 1)

            def turn_probs(n):
                for kind in range(2):
                    wait(pe, scaled[kind], N * b + n + 1)
                    wait(pe, p_copied[kind], N * b + n)
                    for h in range(2):
                        for kt in range(KT):
                            mm = pe.transpose(bank_t[kind][:, (h * KT + kt) * P:(h * KT + kt + 1) * P],
                                              probs[:, kind, n % 3, h, kt * P:(kt + 1) * P], ident)
                    mm.then_inc(p_turned[kind], 1)

            def weigh(n):
                r, g = 32 * (n % 4), n // 4
                c = 2 * XD * (n % PAIRS)
                if n % 4 == 0 and g >= 2:
                    wait(pe, extracted, GROUPS * b + g - 1)
                for kind in range(2):
                    wait(pe, p_copied[kind], N * b + n + 1)
                    for kt in range(KT):
                        mm = pe.matmul(bank_o[g % 2][r:r + 32, 0:2 * P], val[:, kind, kt, c:c + 2 * XD],
                                       probs_t[:, kind, n % 2, :, kt, :], start=(kind == 0 and kt == 0),
                                       stop=(kind == 1 and kt == KT - 1))
                if n % 4 == 3:
                    mm.then_inc(group_done, 1)

            wait(pe, x_copied, 16 * (b + 1))
            wait(pe, y_added, 2 * b)
            project(bank_s[0][0], w_q, 0, x_b)
            project(bank_s[0][1], w_q, 2, x_b).then_inc(q_projected, 1)
            project(bank_s[1][0], w_k, 0, x_b)
            project(bank_s[1][1], w_k, 2, x_b).then_inc(k_projected, 1)
            wait(pe, ctx_loaded, 16 * (b + 1))
            project(bank_t[0], w_k, 0, ctx_b)
            project(bank_t[1], w_k, 2, ctx_b).then_inc(ak_projected, 1)
            wait(pe, q_copied, b + 1)
            for m in range(XT):
                mm = pe.matmul(bank_o[m // 2][:, m % 2 * S:(m % 2 + 1) * S], turn[:, :], q_raw[:, m, :], start=True, stop=True)
            mm.then_inc(q_turned, 1)
            values(bank_s[0][0], 0, x_b)
            values(bank_s[0][1], 1, x_b).then_inc(v_projected, 1)
            wait(pe, k_copied, b + 1)
            for m in range(XT):
                mm = pe.matmul(bank_s[1][m // 2][:, m % 2 * S:(m % 2 + 1) * S], turn[:, :], k_raw[:, m, :], start=True, stop=True)
            mm.then_inc(k_turned, 1)
            wait(pe, ak_copied, b + 1)
            values(bank_t[0], 0, ctx_b)
            values(bank_t[1], 1, ctx_b).then_inc(av_projected, 1)

            wait(pe, q_ready, b + 1)
            wait(pe, k_ready, b + 1)
            wait(pe, v_copied, b + 1)
            score(0)
            wait(pe, av_copied, b + 1)
            for n in range(N + 2):
                if n + 1 < N:
                    score(n + 1)
                if 1 <= n <= N:
                    turn_probs(n - 1)
                if n >= 2:
                    weigh(n - 2)
            wait(pe, extracted, GROUPS * (b + 1))
            for q in range(QT):
                for k in range(KC):
                    mm = pe.matmul(bank_o[q][:, :], attn_t[:, k, q * P:(q + 1) * P], w_o[:, k, :],
                                   start=(k == 0), stop=(k == KC - 1))
                mm.then_inc(y_done, 1)

        def act_batch(act, b):
            def flat(x):
                return x.rearrange("p a n -> p (a n)")

            wait(act, q_projected, b + 1)
            act.activation(flat(q_raw[:, 0:2]), bank_s[0][0][:, :], ACT.Copy, scale=XD ** -0.5)
            act.activation(flat(q_raw[:, 2:4]), bank_s[0][1][:, :], ACT.Copy, scale=XD ** -0.5).then_inc(q_copied, 1)
            wait(act, k_projected, b + 1)
            act.activation(flat(k_raw[:, 0:2]), bank_s[1][0][:, :], ACT.Copy)
            act.activation(flat(k_raw[:, 2:4]), bank_s[1][1][:, :], ACT.Copy).then_inc(k_copied, 1)
            wait(act, ak_projected, b + 1)
            for m in range(0, XT, 2):
                for h in range(2):
                    op = act.activation(ak_pair[:, m:m + 2, h, :], bank_t[m // 2][:].rearrange("p (m n) -> p m n", m=2),
                                        ACT.Copy, scale=halves[:, h:h + 1])
            op.then_inc(ak_copied, 1)
            wait(act, v_projected, b + 1)
            for t in range(KT):
                op = act.activation(val[:, 0, t, :], bank_s[0][t][:, :], ACT.Copy)
            op.then_inc(v_copied, 1)
            wait(act, k_rotated, b + 1)
            for h in range(2):
                op = act.activation(k_pair[:, :, h, :], k_rot[:], ACT.Copy, scale=halves[:, h:h + 1])
            op.then_inc(k_ready, 1)
            wait(act, av_projected, b + 1)
            for t in range(KT):
                op = act.activation(val[:, 1, t, :], bank_t[t][:, :], ACT.Copy)
            op.then_inc(av_copied, 1)

            def exps(n, kind):
                wait(act, topped[kind], N * b + n + 1)
                if n >= 2:
                    wait(act, gained, N * b + n - 1)
                if n >= 3:
                    wait(act, p_turned[kind], N * b + n - 2)
                src = scores[:, n % 2] if kind == 0 else bank_s[1][n % 2][:].rearrange("p (h n) -> p h n", h=2)
                for h in range(2):
                    op = act.activation(probs[:, kind, n % 3, h, :], src[:, h, :], ACT.Exp, bias=top[:, kind, n % 2, h:h + 1],
                                        accum_out=sums[:, n % 2, kind, h:h + 1])
                op.then_inc(exped[kind], 1)

            def copy_turned(n):
                for kind in range(2):
                    wait(act, p_turned[kind], N * b + n + 1)
                    act.activation(probs_t[:, kind, n % 2].rearrange("p h k n -> p (h k n)"), bank_t[kind][:, :], ACT.Copy)\
                        .then_inc(p_copied[kind], 1)

            for n in range(N + 1):
                if n < N:
                    exps(n, 1)
                    exps(n, 0)
                if n > 0:
                    copy_turned(n - 1)

        def dve_batch(v, b):
            def rotate(raw, turned_banks, out, turned, done, base):
                v.tensor_tensor(out[:], raw[:], cos[:, None, :].to_broadcast([P, XT, S]), ALU.mult).then_inc(step, 1)
                wait(v, step, base + 1)
                wait(v, turned, b + 1)
                for m in range(0, XT, 2):
                    v.tensor_tensor(raw[:, m:m + 2], turned_banks[m // 2][:].rearrange("p (m n) -> p m n", m=2),
                                    sin[:, None, :].to_broadcast([P, 2, S]), ALU.mult).then_inc(step, 1)
                wait(v, step, base + 3)
                v.tensor_tensor(out[:], out[:], raw[:], ALU.add).then_inc(done, 1)

            wait(v, mask_loaded, 16 * (b + 1))
            v.tensor_scalar(mask[:], mask_in[:], -3.4028234663852886e38, None, ALU.max).then_inc(mask_guarded, 1)
            wait(v, q_copied, b + 1)
            rotate(q_raw, bank_o, q_rot, q_turned, q_ready, 6 * b)
            wait(v, k_copied, b + 1)
            rotate(k_raw, bank_s[1], k_rot, k_turned, k_rotated, 6 * b + 3)
            wait(v, mask_guarded, b + 1)

            def tops(n):
                q = n // PAIRS
                wait(v, scored[0], N * b + n + 1)
                wait(v, exped[0], N * b + n - 1) if n >= 2 else None
                v.tensor_tensor(scores[:, n % 2], bank_s[0][n % 2][:].rearrange("p (h n) -> p h n", h=2),
                                mask[:, q:q + 1, :].to_broadcast([P, 2, S]), ALU.add).then_inc(masked, 1)
                wait(v, scored[1], N * b + n + 1)
                wait(v, exped[1], N * b + n - 1) if n >= 2 else None
                v.tensor_reduce(top[:, 1, n % 2, :], bank_s[1][n % 2][:].rearrange("p (h n) -> p h n", h=2), AX_X,
                                ALU.max, negate=True).then_inc(topped[1], 1)
                wait(v, masked, N * b + n + 1)
                v.tensor_reduce(top[:, 0, n % 2, :], scores[:, n % 2], AX_X, ALU.max, negate=True).then_inc(topped[0], 1)

            def scale(n):
                for kind in range(2):
                    wait(v, exped[kind], N * b + n + 1)
                if n >= 2:
                    wait(v, scaled[1], N * b + n - 1)
                v.reciprocal(shares[:, n % 2].rearrange("p k h -> p (k h)"), sums[:, n % 2].rearrange("p k h -> p (k h)"))\
                    .then_inc(shared, 1)
                wait(v, shared, N * b + n + 1)
                v.tensor_tensor(shares[:, n % 2], shares[:, n % 2], gains[:, n % PAIRS], ALU.mult).then_inc(gained, 1)
                wait(v, gained, N * b + n + 1)
                for h in range(2):
                    at = probs[:, 0, n % 3, h, :]
                    op = v.tensor_scalar(at, at, shares[:, n % 2, 0, h:h + 1], None, ALU.mult)
                op.then_inc(scaled[0], 1)

            def extract(g):
                q, t = g // XT, g % XT
                wait(v, group_done, GROUPS * b + g + 1)
                wait(v, extracted, GROUPS * b + g)
                v.tensor_scalar(second[:, :], bank_o[g % 2][:, P:2 * P], halves[:, 1:2], None, ALU.mult).then_inc(second_taken, 1)
                wait(v, second_taken, GROUPS * b + g + 1)
                v.scalar_tensor_tensor(out=attn_t[:, t, q * P:(q + 1) * P], in0=bank_o[g % 2][:, 0:P], scalar=halves[:, 0:1],
                                       in1=second[:, :], op0=ALU.mult, op1=ALU.add).then_inc(extracted, 1)

            tops(0)
            for n in range(N):
                if n + 1 < N:
                    tops(n + 1)
                scale(n)
                if n >= 6 and (n - 6) % 4 == 0:
                    extract((n - 6) // 4)
            extract(GROUPS - 1)
            for q in range(QT):
                wait(v, y_done, QT * b + q + 1)
                at = tokens[:, bass.ds(b * QT + q, 1), :]
                v.tensor_tensor(at, at, bank_o[q][:].rearrange("p (o n) -> p o n", o=1), ALU.add).then_inc(y_added, 1)

        with nc.Block() as block:

            @block.sync
            def _(sp):
                for to, source in ((w_q, w_q_dram), (w_k, w_k_dram), (w_v, w_v_dram), (w_o, w_o_dram), (cos, cos_dram),
                                   (sin, sin_dram), (turn, turn_dram), (halves, halves_dram), (gate_in, tanh_gate_src)):
                    sp.dma_start(to[:], source).then_inc(consts, 16)
                sp.wait_ge(consts, 16 * 9)

                def batch(b):
                    wait(sp, av_projected, b)
                    wait(sp, mask_guarded, b)
                    wait(sp, consts, 16 * 9)
                    sp.dma_start(x_b[:], x_t[:, :, bass.ds(b * S, S)]).then_inc(x_copied, 16)
                    sp.dma_start(ctx_b[:], ctx_dram[:, :, bass.ds(b * S, S)]).then_inc(ctx_loaded, 16)
                    sp.dma_start(mask_in[:], mask_dram[bass.ds(b, 1)].rearrange("o p q k -> (o p) q k")).then_inc(mask_loaded, 16)

                batch(0)
                with sp.Fori(1, B) as b:
                    batch(b)

            @block.tensor
            def _(pe):
                pe.wait_ge(consts, 16 * 9)
                pe_batch(pe, 0)
                with pe.Fori(1, B) as b:
                    pe_batch(pe, b)

            @block.scalar
            def _(act):
                act.wait_ge(consts, 16 * 9)
                act.wait_ge(gains_set, 1)
                act.activation(gains[:, :, 1, :], gate_in[:].rearrange("p (a h) -> p a h", h=2), ACT.Tanh).then_inc(gate_made, 1)
                act_batch(act, 0)
                with act.Fori(1, B) as b:
                    act_batch(act, b)

            @block.vector
            def _(v):
                v.wait_ge(consts, 16 * 9)
                v.memset(gains[:], 1.0).then_inc(gains_set, 1)
                v.wait_ge(gate_made, 1)
                dve_batch(v, 0)
                with v.Fori(1, B) as b:
                    dve_batch(v, b)
                v.wait_ge(y_added, QT * B)

            @block.gpsimd
            def _(g):
                def scale_batch(b):
                    for n in range(N):
                        wait(g, gained, N * b + n + 1)
                        at = probs[:, 1, n % 3]
                        g.tensor_tensor(at, at, shares[:, n % 2, 1, :, None].to_broadcast([P, 2, S]), ALU.mult)\
                            .then_inc(scaled[1], 1)

                scale_batch(0)
                with g.Fori(1, B) as b:
                    scale_batch(b)


SEL = S // 8
ROWS = B * SEL
RT = ROWS // P
BT = B // RT
FH, FKV, FD = 16, 8, 128
FI = 2048
FF_EPS = 1e-6
LOWEST = -3.4028234663852886e38


def select_phase(nc, tokens, w_router_dram, before_dram, counts_dram, tables_dram, ident, rows, angles, row_scores,
                 pick_t, junk):
    with ExitStack() as stack:
        a = Space(nc, stack, "se_")
        w_router = a.sb("w_router", [P, D])
        before = a.sb("before", [P, NC, S])
        counts = a.sb("counts", [P, SEL])
        earlier = a.sb("earlier", [P, P])
        table = a.sb("table", [P, NC, P])
        ones = a.sb("ones", [P, P])
        score = a.sb("score", [P, NT])
        diag = a.sb("diag", [P, NT, P])
        score_rows = a.sb("score_rows", [P, NT, P])
        score_own = a.sb("score_own", [P, NT])
        ties = a.sb("ties", [P, NT, S])
        rank = a.sb("rank", [P, NT])
        chosen = a.sb("chosen", [P, NT])
        chosen_before = a.sb("chosen_before", [P, B, NC])
        slot = a.sb("slot", [P, NT])
        pick = a.sb("pick", [P, NC, B, SEL])
        banks = [a.bank(f"b{n}") for n in range(8)]
        loaded, ones_made, step = a.sem("loaded"), a.sem("ones_made"), a.sem("step")
        diag_made, spread, spread_copied = a.sem("diag_made"), a.sem("spread"), a.sem("spread_copied")
        chosen_made, counted, pick_made = a.sem("chosen_made"), a.sem("counted"), a.sem("pick_made")
        gathered, gathered_copied, picks_turned = a.sem("gathered"), a.sem("gathered_copied"), a.sem("picks_turned")
        with nc.Block() as block:

            @block.sync
            def _(sp):
                for to, source in ((w_router[:], w_router_dram), (before[:], before_dram),
                                   (counts[:], counts_dram[:, 0:SEL]), (earlier[:], counts_dram[:, SEL:SEL + P]),
                                   (table[:], tables_dram)):
                    sp.dma_start(to, source).then_inc(loaded, 16)

            @block.tensor
            def _(pe):
                pe.wait_ge(ones_made, 1)
                pe.wait_ge(diag_made, 1)
                for n in range(4):
                    mm = pe.matmul(banks[n][:, :], ones[:, :], diag[:, 4 * n:4 * n + 4].rearrange("p t n -> p (t n)"),
                                   start=True, stop=True)
                mm.then_inc(spread, 1)
                pe.wait_ge(chosen_made, 1)
                pe.matmul(banks[4][:, 0:NT], earlier[:, :], chosen[:, :], start=True, stop=False)
                pe.matmul(banks[4][:, 0:NT], ones[:, :], chosen_before[:].rearrange("p b c -> p (b c)"),
                          start=False, stop=True).then_inc(counted, 1)
                pe.wait_ge(pick_made, 1)
                pe.wait_ge(spread_copied, 1)
                for b in range(B):
                    r, q = b // BT, SEL * (b % BT)
                    for c in range(NC):
                        flags = dict(start=(c == 0), stop=(c == NC - 1))
                        pe.matmul(banks[r][q:q + SEL, :], pick[:, c, b, :], tokens[:, NC * b + c, :], **flags)
                    for c in range(NC):
                        flags = dict(start=(c == 0), stop=(c == NC - 1))
                        pe.matmul(banks[2 + r][q:q + SEL, 0:P], pick[:, c, b, :], table[:, c, :], **flags)
                    for c in range(NC):
                        flags = dict(start=(c == 0), stop=(c == NC - 1))
                        mm = pe.matmul(banks[5 + r][q:q + SEL, 0:1], pick[:, c, b, :],
                                       score_own[:, NC * b + c:NC * b + c + 1], **flags)
                mm.then_inc(gathered, 1)
                for r in range(RT):
                    for c in range(NC):
                        mm = pe.transpose(banks[7][:, (r * NC + c) * P:(r * NC + c + 1) * P],
                                          pick[:, c, BT * r:BT * (r + 1), :].rearrange("p b n -> p (b n)"), ident)
                mm.then_inc(picks_turned, 1)

            @block.scalar
            def _(act):
                act.wait_ge(spread, 1)
                for n in range(4):
                    op = act.activation(score_rows[:, 4 * n:4 * n + 4].rearrange("p t n -> p (t n)"), banks[n][:, :], ACT.Copy)
                op.then_inc(spread_copied, 1)
                act.wait_ge(gathered, 1)
                for r in range(RT):
                    act.activation(rows[:, r, :], banks[r][:, :], ACT.Copy)
                    act.activation(angles[:, r, :], banks[2 + r][:, 0:P], ACT.Copy)
                    act.activation(row_scores[:, r:r + 1], banks[5 + r][:, 0:1], ACT.Copy)
                act.wait_ge(picks_turned, 1)
                act.activation(pick_t[:].rearrange("p r c n -> p (r c n)"), banks[7][:, :], ACT.Copy).then_inc(gathered_copied, 1)
                act.wait_ge(gathered_copied, 1)

            @block.vector
            def _(v):
                n = 0

                def then(op):
                    nonlocal n
                    n += 1
                    op.then_inc(step, 1)
                    v.wait_ge(step, n)

                v.memset(ones[:], 1.0).then_inc(ones_made, 1)
                v.memset(chosen_before[:], 0.0)
                v.wait_ge(loaded, 80)
                for t in range(NT):
                    op = v.tensor_tensor_reduce(out=junk[:, t, :], in0=tokens[:, t, :], in1=w_router[:, :], scale=1.0,
                                                scalar=0.0, op0=ALU.mult, op1=ALU.add, accum_out=score[:, t:t + 1])
                then(op)
                v.tensor_tensor(diag[:], ident[:, None, :].to_broadcast([P, NT, P]),
                                score[:, :, None].to_broadcast([P, NT, P]), ALU.mult).then_inc(diag_made, 1)
                v.wait_ge(spread_copied, 1)
                for t in range(NT):
                    op = v.tensor_tensor_reduce(out=junk[:, t, 0:P], in0=score_rows[:, t, :], in1=ident, scale=1.0,
                                                scalar=0.0, op0=ALU.mult, op1=ALU.add, accum_out=score_own[:, t:t + 1])
                then(op)
                for t in range(NT):
                    batch = score_rows[:, t - t % NC:t - t % NC + NC].rearrange("p c n -> p (c n)")
                    op = v.scalar_tensor_tensor(out=ties[:, t, :], in0=batch, scalar=score_own[:, t:t + 1],
                                                in1=before[:, t % NC, :], op0=ALU.is_equal, op1=ALU.mult)
                then(op)
                for t in range(NT):
                    batch = score_rows[:, t - t % NC:t - t % NC + NC].rearrange("p c n -> p (c n)")
                    op = v.scalar_tensor_tensor(out=ties[:, t, :], in0=batch, scalar=score_own[:, t:t + 1],
                                                in1=ties[:, t, :], op0=ALU.is_gt, op1=ALU.add)
                then(op)
                then(v.tensor_reduce(rank[:, :], ties[:], AX_X, ALU.add))
                then(v.tensor_scalar(chosen[:, :], rank[:, :], float(SEL), None, ALU.is_lt))
                v.tensor_copy(chosen_before[:, :, 1], chosen[:].rearrange("p (b c) -> p b c", c=NC)[:, :, 0])\
                    .then_inc(chosen_made, 1)
                v.wait_ge(counted, 1)
                then(v.tensor_copy(slot[:, :], banks[4][:, 0:NT]))
                for c in range(NC):
                    op = v.tensor_tensor(pick[:, c], counts[:, None, :].to_broadcast([P, B, SEL]),
                                         slot[:].rearrange("p (b c) -> p c b", c=NC)[:, c, :, None].to_broadcast([P, B, SEL]),
                                         ALU.is_equal)
                then(op)
                for c in range(NC):
                    op = v.tensor_tensor(pick[:, c], pick[:, c],
                                         chosen[:].rearrange("p (b c) -> p c b", c=NC)[:, c, :, None].to_broadcast([P, B, SEL]),
                                         ALU.mult)
                op.then_inc(pick_made, 1)


def rms_turn(nc, block, a, x, weight, out_t, ident, banks, ready=None):
    junk = a.sb("rt_junk", [P, RT, D])
    sumsq, den = a.sb("rt_sumsq", [P, RT]), a.sb("rt_den", [P, RT])
    eps = a.sb("rt_eps", [P, 1])
    normed = a.sb("rt_normed", [P, RT, D])
    eps_made, squared, rooted = a.sem("rt_eps_made"), a.sem("rt_squared"), a.sem("rt_rooted")
    inverted, scaled, turned, copied = a.sem("rt_inverted"), a.sem("rt_scaled"), a.sem("rt_turned"), a.sem("rt_copied")

    @block.vector
    def _(v):
        v.memset(eps[:], FF_EPS).then_inc(eps_made, 1)
        v.wait_ge(rooted, 1)
        v.reciprocal(den[:, :], den[:, :]).then_inc(inverted, 1)
        v.wait_ge(inverted, 1)
        for r in range(RT):
            op = v.tensor_scalar(normed[:, r, :], x[:, r, :], den[:, r:r + 1], None, ALU.mult)
        op.then_inc(scaled, 1)

    @block.tensor
    def _(pe):
        pe.wait_ge(scaled, 1)
        for k in range(KC):
            for r in range(RT):
                at = (k % 2 * RT + r) * P
                mm = pe.transpose(banks[k // 2][:, at:at + P], normed[:, r, k * P:(k + 1) * P], ident)
        mm.then_inc(turned, 1)

    @block.scalar
    def _(act):
        act.wait_ge(eps_made, 1)
        for r in range(RT):
            op = act.activation(junk[:, r, :], x[:, r, :], ACT.Square, accum_out=sumsq[:, r:r + 1])
        op.then_inc(squared, 1)
        act.wait_ge(squared, 1)
        act.activation(den[:, :], sumsq[:, :], ACT.Sqrt, scale=1.0 / D, bias=eps[:, 0:1]).then_inc(rooted, 1)
        act.wait_ge(turned, 1)
        for k in range(KC):
            op = act.activation(out_t[:, k, :], banks[k // 2][:, k % 2 * ROWS:(k % 2 + 1) * ROWS], ACT.Copy,
                                scale=weight[:, k:k + 1])
        op.then_inc(copied, 1)
        act.wait_ge(copied, 1)


def ffn_phase(nc, tokens, w_router_dram, before_dram, counts_dram, tables_dram, causal_dram, ln_dram, bias_dram,
              w_qkv_dram, w_o_dram, w_gu_dram, w_down_dram, ident):
    with ExitStack() as stack:
        a = Space(nc, stack, "ff_")
        wide = a.sb("wide", [P, KC, 4096])
        tall = a.sb("tall", [P, FI // P, D])
        ln = a.sb("ln", [P, 2, KC])
        causal = a.sb("causal", [P, RT, ROWS])
        rows = a.sb("rows", [P, RT, D])
        angles = a.sb("angles", [P, RT, P])
        row_scores = a.sb("row_scores", [P, RT])
        pick_t = a.sb("pick_t", [P, RT, NC, P])
        update = a.sb("update", [P, RT, D])
        x_mid = a.sb("x_mid", [P, RT, D])
        h_t = a.sb("h_t", [P, KC, ROWS])
        sem = a.sem
        small_loaded, qkv_loaded, bias_loaded, o_loaded = sem("small_loaded"), sem("qkv_loaded"), sem("bias_loaded"), sem("o_loaded")
        gu_loaded, down_loaded = sem("gu_loaded"), sem("down_loaded")

        with nc.Block() as block:

            @block.sync
            def _(sp):
                sp.dma_start(ln[:], ln_dram).then_inc(small_loaded, 16)
                sp.dma_start(causal[:], causal_dram).then_inc(small_loaded, 16)
                sp.dma_start(wide[:], w_qkv_dram).then_inc(qkv_loaded, 16)
                sp.wait_ge(small_loaded, 32)

        select_phase(nc, tokens, w_router_dram, before_dram, counts_dram, tables_dram, ident, rows, angles,
                     row_scores, pick_t, tall)

        with ExitStack() as attention:
            t = Space(nc, attention, "fa_")
            q_t = t.sb("q_t", [P, FH, ROWS])
            k_t = t.sb("k_t", [P, FKV, ROWS])
            val = t.sb("val", [P, RT, FKV * FD])

            with ExitStack() as scope:
                b1 = Space(nc, scope, "f1_")
                banks = [b1.bank(f"b{n}") for n in range(2)]
                with nc.Block() as block:
                    rms_turn(nc, block, b1, rows, ln[:, 0], h_t, ident, banks)

            with ExitStack() as scope:
                b2 = Space(nc, scope, "f2_")
                bias = tall[:, 0:8, :].rearrange("p m n -> p (m n)")
                raw = b2.sb("raw", [P, 2, D])
                by_cos, by_sin = b2.sb("by_cos", [P, 2, D]), b2.sb("by_sin", [P, 2, D])
                rotated = b2.sb("rotated", [P, 2, D])
                banks = [b2.bank(f"b{n}") for n in range(2)]
                banks_t = [b2.bank(f"t{n}") for n in range(2)]
                projected, biased, turned_in, turned, copied = (b2.sem(n) for n in (
                    "projected", "biased", "rotary_done", "turned", "copied"))
                multiplied = b2.sem("multiplied")
                STEPS = [(m, r) for m in range(8) for r in range(RT)]
                TURNED = 6 * RT
                with nc.Block() as block:

                    @block.sync
                    def _(sp):
                        sp.dma_start(bias, bias_dram.partition_broadcast(P)).then_inc(bias_loaded, 16)

                    @block.tensor
                    def _(pe):
                        def turn(n):
                            pe.wait_ge(turned_in, n + 1)
                            wait(pe, copied, n - 1)
                            for h in range(4):
                                mm = pe.transpose(banks_t[n % 2][:, h * P:(h + 1) * P],
                                                  rotated[:, n % 2, h * P:(h + 1) * P], ident)
                            mm.then_inc(turned, 1)

                        pe.wait_ge(qkv_loaded, 16)
                        for n, (m, r) in enumerate(STEPS):
                            wait(pe, biased, n - 1)
                            for k in range(KC):
                                mm = pe.matmul(banks[n % 2][:, :], h_t[:, k, r * P:(r + 1) * P],
                                               wide[:, k, m * D:(m + 1) * D], start=(k == 0), stop=(k == KC - 1))
                            mm.then_inc(projected, 1)
                            if 1 <= n <= TURNED:
                                turn(n - 1)

                    @block.vector
                    def _(v):
                        v.wait_ge(bias_loaded, 16)
                        for n, (m, r) in enumerate(STEPS):
                            v.wait_ge(projected, n + 1)
                            if n < TURNED:
                                out = raw[:, n % 2, :]
                                wait(v, multiplied, 3 * (n - 1))
                            else:
                                out = val[:, r, (m - 6) * D:(m - 5) * D]
                            v.tensor_tensor(out, banks[n % 2][:, :], bias[:, m * D:(m + 1) * D], ALU.add).then_inc(biased, 1)
                            if n >= TURNED:
                                continue
                            v.wait_ge(biased, n + 1)
                            wait(v, turned_in, n - 1)
                            x4 = raw[:, n % 2].rearrange("p (h a d) -> p h a d", h=4, a=2)
                            s4 = by_sin[:, n % 2].rearrange("p (h a d) -> p h a d", h=4, a=2)
                            cos = angles[:, r, None, 0:64].to_broadcast([P, 8, 64])
                            sin = angles[:, r, None, 64:128].to_broadcast([P, 4, 64])
                            v.tensor_tensor(by_cos[:, n % 2].rearrange("p (h d) -> p h d", d=64),
                                            raw[:, n % 2].rearrange("p (h d) -> p h d", d=64), cos, ALU.mult).then_inc(multiplied, 1)
                            v.tensor_tensor(s4[:, :, 0], x4[:, :, 1], sin, ALU.mult).then_inc(multiplied, 1)
                            v.tensor_tensor(s4[:, :, 1], x4[:, :, 0], sin, ALU.mult).then_inc(multiplied, 1)
                            v.wait_ge(multiplied, 3 * (n + 1))
                            wait(v, turned, n - 1)
                            c4 = by_cos[:, n % 2].rearrange("p (h a d) -> p h a d", h=4, a=2)
                            r4 = rotated[:, n % 2].rearrange("p (h a d) -> p h a d", h=4, a=2)
                            v.tensor_tensor(r4[:, :, 0], c4[:, :, 0], s4[:, :, 0], ALU.subtract)
                            v.tensor_tensor(r4[:, :, 1], c4[:, :, 1], s4[:, :, 1], ALU.add).then_inc(turned_in, 1)
                        v.wait_ge(biased, len(STEPS))

                    @block.scalar
                    def _(act):
                        for n, (m, r) in enumerate(STEPS[:TURNED]):
                            act.wait_ge(turned, n + 1)
                            to = q_t[:, 4 * m:4 * m + 4] if m < 4 else k_t[:, 4 * (m - 4):4 * (m - 3)]
                            act.activation(to[:, :, r * P:(r + 1) * P], banks_t[n % 2][:].rearrange("p (h n) -> p h n", h=4),
                                           ACT.Copy).then_inc(copied, 1)
                        act.wait_ge(copied, TURNED)

            with ExitStack() as scope:
                b3 = Space(nc, scope, "f3_")
                o_t = q_t
                masked = b3.sb("masked", [P, 2, RT, ROWS])
                top = b3.sb("top", [P, 2, RT])
                probs = b3.sb("probs", [P, 2, RT, ROWS])
                sums = b3.sb("sums", [P, 2, RT])
                inv = b3.sb("inv", [P, 2, RT])
                probs_t = b3.sb("probs_t", [P, 2, 3, P])
                banks_s = [b3.bank(f"s{n}") for n in range(2)]
                banks_t = [b3.bank(f"t{n}") for n in range(2)]
                banks_o = [b3.bank(f"o{n}") for n in range(2)]
                banks_y = [b3.bank(f"y{n}") for n in range(2)]
                scored, masked_s, topped, exped, inverted, scaled, turned, copied, weighed, o_copied, y_done, y_copied = (
                    b3.sem(n) for n in ("scored", "masked_done", "topped", "exped", "inverted", "scaled", "turned",
                                        "copied", "weighed", "o_copied", "y_done", "y_copied"))
                with nc.Block() as block:

                    @block.sync
                    def _(sp):
                        sp.dma_start(tall[:], w_o_dram).then_inc(o_loaded, 16)
                        sp.dma_start(wide[:], w_gu_dram).then_inc(gu_loaded, 16)
                        sp.wait_ge(y_done, 1)
                        sp.dma_start(tall[:], w_down_dram).then_inc(down_loaded, 16)

                    @block.tensor
                    def _(pe):
                        def score(h):
                            wait(pe, masked_s, h - 1)
                            for r in range(RT):
                                mm = pe.matmul(banks_s[h % 2][:, r * ROWS:r * ROWS + (r + 1) * P],
                                               q_t[:, h, r * P:(r + 1) * P], k_t[:, h // 2, 0:(r + 1) * P],
                                               start=True, stop=True)
                            mm.then_inc(scored, 1)

                        def turn(h):
                            pe.wait_ge(scaled, h + 1)
                            wait(pe, copied, h - 1)
                            for n, (r, c) in enumerate(((0, 0), (1, 0), (1, 1))):
                                mm = pe.transpose(banks_t[h % 2][:, n * P:(n + 1) * P], probs[:, h % 2, r, c * P:(c + 1) * P], ident)
                            mm.then_inc(turned, 1)

                        def weigh(h):
                            pe.wait_ge(copied, h + 1)
                            wait(pe, o_copied, h - 1)
                            g = h // 2 * FD
                            pe.matmul(banks_o[h % 2][:, 0:ROWS], val[:, 0, g:g + FD],
                                      probs_t[:, h % 2, 0:2].rearrange("p r n -> p (r n)"), start=True, stop=False,
                                      skip_group_check=True)
                            pe.matmul(banks_o[h % 2][:, P:ROWS], val[:, 1, g:g + FD], probs_t[:, h % 2, 2],
                                      start=False, stop=True, skip_group_check=True).then_inc(weighed, 1)

                        score(0)
                        for h in range(FH):
                            if h + 1 < FH:
                                score(h + 1)
                            if h > 0:
                                weigh(h - 1)
                            turn(h)
                        weigh(FH - 1)
                        pe.wait_ge(o_loaded, 16)
                        pe.wait_ge(o_copied, FH)
                        for r in range(RT):
                            for k in range(FH):
                                mm = pe.matmul(banks_y[r][:, :], o_t[:, k, r * P:(r + 1) * P], tall[:, k, :],
                                               start=(k == 0), stop=(k == FH - 1))
                        mm.then_inc(y_done, 1)

                    @block.vector
                    def _(v):
                        def tops(h):
                            v.wait_ge(scored, h + 1)
                            wait(v, exped, h - 1)
                            for r in range(RT):
                                w = (r + 1) * P
                                op = v.scalar_tensor_tensor(out=masked[:, h % 2, r, 0:w], in0=banks_s[h % 2][:, r * ROWS:r * ROWS + w],
                                                            scalar=FD ** -0.5, in1=causal[:, r, 0:w], op0=ALU.mult, op1=ALU.add)
                            op.then_inc(masked_s, 1)
                            v.wait_ge(masked_s, h + 1)
                            for r in range(RT):
                                op = v.tensor_reduce(top[:, h % 2, r:r + 1], masked[:, h % 2, r, 0:(r + 1) * P], AX_X,
                                                     ALU.max, negate=True)
                            op.then_inc(topped, 1)

                        def scale(h):
                            v.wait_ge(exped, h + 1)
                            v.reciprocal(inv[:, h % 2, :], sums[:, h % 2, :]).then_inc(inverted, 1)
                            v.wait_ge(inverted, h + 1)
                            for r in range(RT):
                                w = (r + 1) * P
                                op = v.tensor_scalar(probs[:, h % 2, r, 0:w], probs[:, h % 2, r, 0:w], inv[:, h % 2, r:r + 1],
                                                     None, ALU.mult)
                            op.then_inc(scaled, 1)

                        tops(0)
                        for h in range(FH):
                            if h + 1 < FH:
                                tops(h + 1)
                            scale(h)
                            v.wait_ge(turned, h + 1)
                            v.tensor_copy(probs_t[:, h % 2].rearrange("p n m -> p (n m)"), banks_t[h % 2][:, 0:3 * P])\
                                .then_inc(copied, 1)
                        v.wait_ge(y_done, 1)
                        for r in range(RT):
                            op = v.tensor_tensor(x_mid[:, r, :], rows[:, r, :], banks_y[r][:, :], ALU.add)
                        for r in range(RT):
                            op = v.tensor_copy(update[:, r, :], banks_y[r][:, :])
                        op.then_inc(y_copied, 1)
                        v.wait_ge(y_copied, 1)

                    @block.scalar
                    def _(act):
                        for h in range(FH):
                            act.wait_ge(topped, h + 1)
                            wait(act, turned, h - 1)
                            for r in range(RT):
                                w = (r + 1) * P
                                op = act.activation(probs[:, h % 2, r, 0:w], masked[:, h % 2, r, 0:w], ACT.Exp,
                                                    bias=top[:, h % 2, r:r + 1], accum_out=sums[:, h % 2, r:r + 1])
                            op.then_inc(exped, 1)
                            if h > 0:
                                act.wait_ge(weighed, h)
                                act.activation(o_t[:, h - 1, :], banks_o[(h - 1) % 2][:, 0:ROWS], ACT.Copy).then_inc(o_copied, 1)
                        act.wait_ge(weighed, FH)
                        act.activation(o_t[:, FH - 1, :], banks_o[(FH - 1) % 2][:, 0:ROWS], ACT.Copy).then_inc(o_copied, 1)

        with ExitStack() as scope:
            b4 = Space(nc, scope, "f4_")
            banks = [b4.bank(f"b{n}") for n in range(2)]
            with nc.Block() as block:
                rms_turn(nc, block, b4, x_mid, ln[:, 1], h_t, ident, banks)
        with ExitStack() as scope:
            b5 = Space(nc, scope, "f5_")
            act_t = b5.sb("act_t", [P, FI // P, ROWS])
            gate = b5.sb("gate", [P, 2, ROWS])
            row_gate = b5.sb("row_gate", [P, RT])
            banks = [b5.bank(f"b{n}") for n in range(4)]
            banks_y = [b5.bank(f"y{n}") for n in range(4)]
            projected, silued, multiplied = b5.sem("projected"), b5.sem("silued"), b5.sem("multiplied")
            y_done, gate_made, summed, updated = b5.sem("y_done"), b5.sem("gate_made"), b5.sem("summed"), b5.sem("updated")
            scattered, added = b5.sem("scattered"), b5.sem("added")
            MT = FI // P
            with nc.Block() as block:

                @block.tensor
                def _(pe):
                    pe.wait_ge(gu_loaded, 16)
                    for m in range(MT):
                        wait(pe, multiplied, m - 3)
                        for half in range(2):
                            for k in range(KC):
                                mm = pe.matmul(banks[m % 4][:, half * ROWS:(half + 1) * ROWS],
                                               wide[:, k, half * FI + m * P:half * FI + (m + 1) * P], h_t[:, k, :],
                                               start=(k == 0), stop=(k == KC - 1))
                        mm.then_inc(projected, 1)
                    pe.wait_ge(down_loaded, 16)
                    for r in range(RT):
                        for m in range(MT):
                            if r == 0:
                                pe.wait_ge(multiplied, m + 1)
                            mm = pe.matmul(banks_y[r][:, :], act_t[:, m, r * P:(r + 1) * P], tall[:, m, :],
                                           start=(m == 0), stop=(m == MT - 1))
                    mm.then_inc(y_done, 1)
                    pe.wait_ge(updated, 1)
                    for t in range(NT):
                        b, c = t // NC, t % NC
                        q = SEL * (b % BT)
                        wait(pe, added, t - 3)
                        pe.matmul(banks[t % 4][:, :], pick_t[q:q + SEL, b // BT, c, :], update[q:q + SEL, b // BT, :],
                                  start=True, stop=True).then_inc(scattered, 1)

                @block.scalar
                def _(act):
                    act.activation(row_gate[:, :], row_scores[:, :], ACT.Sigmoid).then_inc(gate_made, 1)
                    for m in range(MT):
                        act.wait_ge(projected, m + 1)
                        wait(act, multiplied, m - 1)
                        act.activation(gate[:, m % 2, :], banks[m % 4][:, 0:ROWS], ACT.Silu).then_inc(silued, 1)

                @block.vector
                def _(v):
                    for m in range(MT):
                        v.wait_ge(silued, m + 1)
                        v.tensor_tensor(act_t[:, m, :], gate[:, m % 2, :], banks[m % 4][:, ROWS:2 * ROWS], ALU.mult)\
                            .then_inc(multiplied, 1)
                    v.wait_ge(y_done, 1)
                    for r in range(RT):
                        op = v.tensor_tensor(update[:, r, :], update[:, r, :], banks_y[r][:, :], ALU.add)
                    op.then_inc(summed, 1)
                    v.wait_ge(summed, 1)
                    v.wait_ge(gate_made, 1)
                    for r in range(RT):
                        op = v.tensor_scalar(update[:, r, :], update[:, r, :], row_gate[:, r:r + 1], None, ALU.mult)
                    op.then_inc(updated, 1)
                    for t in range(NT):
                        v.wait_ge(scattered, t + 1)
                        v.scalar_tensor_tensor(out=tokens[:, t, :], in0=tokens[:, t, :], scalar=2.0, in1=banks[t % 4][:, :],
                                               op0=ALU.mult, op1=ALU.add).then_inc(added, 1)
                    v.wait_ge(added, NT)

def host_delta(i):
    f = lambda a: np.ascontiguousarray(a)
    wq = i["L0_attn_w_qkv"]
    parts = [wq[0:1024].reshape(8, 1, 128, 512), wq[1024:2048].reshape(8, 1, 128, 512),
             wq[2048:].reshape(8, 2, 128, 512), i["L0_attn_w_gate"].reshape(8, 2, 128, 512)]
    w = np.concatenate(parts, 1)
    w = w.reshape(8, 768, 4, 128).transpose(0, 3, 2, 1)
    cw = i["L0_attn_conv_w"].reshape(4096, 4)
    cw = np.concatenate([cw[0:1024].reshape(8, 1, 128, 4), cw[1024:2048].reshape(8, 1, 128, 4),
                         cw[2048:].reshape(8, 2, 128, 4)], 1).transpose(0, 2, 1, 3)
    wo = i["L0_attn_w_out"].T.reshape(8, 2, 128, 512).transpose(0, 2, 1, 3)
    wba = np.concatenate([i["L0_attn_w_beta"], i["L0_attn_w_alpha"]], 0).T.reshape(4, 128, 32).transpose(1, 0, 2)
    x = i["x"].reshape(2048, 512)
    return dict(
        x_tok=f(x.reshape(16, 128, 512).transpose(1, 0, 2)), x_t=f(x.T.reshape(4, 128, 2048).transpose(1, 0, 2)),
        w_in=f(w), conv_w=f(cw), w_out=f(wo), w_ba=f(wba),
        rms_w=f(i["L0_attn_rms_w"].reshape(128, 1)),
        log_a=f(np.broadcast_to(i["L0_attn_log_A"], (128, 16))), dt_bias=f(np.broadcast_to(i["L0_attn_dt_bias"], (128, 16))))


def delta_constants():
    r, c = np.indices((128, 128))
    neg_first = -((r // 2 == c // 2) & (r < c)).astype(np.float32)
    joins = np.stack([((r >> (s + 1)) == (c >> (s + 1))) & (((r >> s) & 1) == 1) & (((c >> s) & 1) == 0)
                      for s in range(1, 7)], 1).astype(np.float32)
    return dict(ident=np.eye(128, dtype=np.float32),
                neg_first=np.ascontiguousarray(np.broadcast_to(neg_first[:, None, :], (128, 2, 128))), joins=joins)


def host_cross(i):
    f = lambda a: np.ascontiguousarray(a)
    w = lambda n: f(i[n].reshape(4, 128, 512).transpose(1, 0, 2))
    return dict(
        xw_q=w("L0_xattn_Wq"), xw_k=w("L0_xattn_Wk"), xw_v=w("L0_xattn_Wv"), xw_o=w("L0_xattn_Wo"),
        ctx_t=f(i["ctx_2048"].reshape(2048, 512).T.reshape(4, 128, 2048).transpose(1, 0, 2)),
        mask=f(i["mask_Bx1xSxS_fk0"].reshape(8, 2, 128, 256).transpose(0, 2, 1, 3)),
        x_gate=f(np.broadcast_to(i["L0_xattn_gate"].reshape(1, 32), (128, 32))))


def cross_constants():
    inv_freq = 1.0 / 10000.0 ** (np.arange(0, 16, 2, dtype=np.float32) / 16)
    freqs = np.outer(np.arange(256, dtype=np.float32), inv_freq)
    emb = np.concatenate([freqs, freqs], -1)
    cos, sin = (np.ascontiguousarray(np.tile(t(emb).T, (8, 1)).astype(np.float32)) for t in (np.cos, np.sin))
    turn = np.zeros((128, 128), np.float32)
    for m in range(128):
        if m % 16 < 8:
            turn[m + 8, m] = -1
        else:
            turn[m - 8, m] = 1
    r = np.arange(128)
    halves = np.stack([r % 32 < 16, r % 32 >= 16], 1).astype(np.float32)
    return dict(x_cos=cos, x_sin=sin, x_turn=turn, x_halves=halves)


def host_ffn(i):
    f = lambda a: np.ascontiguousarray(a)
    w = lambda a: f(a.reshape(-1, 128, a.shape[1]).transpose(1, 0, 2))
    return dict(
        w_router=f(np.broadcast_to(i["L0_ffn_w_router"], (128, 512))),
        fw_qkv=w(np.concatenate([i["L0_ffn_wq"], i["L0_ffn_wk"], i["L0_ffn_wv"]], 1)),
        f_bias=f(np.concatenate([i["L0_ffn_bq"], i["L0_ffn_bk"], i["L0_ffn_bv"]])),
        fw_o=w(i["L0_ffn_wo"]), fw_gu=w(np.concatenate([i["L0_ffn_w_gate"], i["L0_ffn_w_up"]], 1)),
        fw_down=w(i["L0_ffn_w_down"]),
        f_ln=f(np.stack([i["L0_ffn_ln1_w"].reshape(4, 128).T, i["L0_ffn_ln2_w"].reshape(4, 128).T], 1)))


def ffn_constants():
    p = np.arange(128)
    pos = np.arange(256)
    before = np.stack([(pos[None, :] < (p + 128 * c)[:, None]) for c in range(2)], 1).astype(np.float32)
    counts = np.concatenate([np.broadcast_to(np.arange(32), (128, 32)), p[:, None] < p[None, :]], 1).astype(np.float32)
    inv_freq = (1.0 / np.float32(10000.0) ** (np.arange(0, 128, 2, dtype=np.float32) / np.float32(128))).astype(np.float32)
    ang = pos.astype(np.float32)[:, None] * inv_freq
    table = np.concatenate([np.cos(ang), np.sin(ang)], 1).astype(np.float32).reshape(2, 128, 128).transpose(1, 0, 2)
    causal = np.where(pos[None, :] <= pos[:, None], 0.0, np.finfo(np.float32).min).astype(np.float32)
    return dict(before=before, counts=np.ascontiguousarray(counts), f_table=np.ascontiguousarray(table),
                causal=np.ascontiguousarray(causal.reshape(2, 128, 256).transpose(1, 0, 2)))


def build_program(nc, d, alpha_dram, out):
    with ExitStack() as stack:
        a = Space(nc, stack, "")
        tokens = a.sb("tokens", [P, NT, D])
        ident = a.sb("ident", [P, P])
        with ExitStack() as turned:
            t = Space(nc, turned, "")
            x_t = t.sb("x_t", [P, KC, TOK])
            with ExitStack() as delta:
                s = Space(nc, delta, "")
                neg_first = s.sb("neg_first", [P, NC, P])
                joins = s.sb("joins", [P, LEVELS - 1, P])
                beta_cols = s.sb("beta_cols", [P, NT * NH])
                load_phase(nc, [(x_t[:], d["x_t"]), (tokens[:], d["x_tok"]), (ident[:], d["ident"]),
                                (neg_first[:], d["neg_first"]), (joins[:], d["joins"])])
                decay_phase(nc, x_t, d["w_ba"], d["log_a"], d["dt_bias"], ident[:], beta_cols[:], alpha_dram)
                delta_phase(nc, tokens, x_t, d["w_in"], d["conv_w"], d["w_out"], d["rms_w"], ident[:],
                            (neg_first[:], joins), beta_cols, alpha_dram.rearrange("(u a) m -> u (a m)", a=VH * NC))
            norm_phase(nc, "ln1", tokens, ident=ident[:], turned=x_t)
            cross_phase(nc, tokens, x_t, d["ctx_t"], d["mask"], [d["xw_q"], d["xw_k"], d["xw_v"], d["xw_o"]],
                        d["x_gate"], [d["x_cos"], d["x_sin"], d["x_turn"], d["x_halves"]], ident[:])
        norm_phase(nc, "ln2", tokens)
        ffn_phase(nc, tokens, d["w_router"], d["before"], d["counts"], d["f_table"], d["causal"], d["f_ln"],
                  d["f_bias"], d["fw_qkv"], d["fw_o"], d["fw_gu"], d["fw_down"], ident[:])
        norm_phase(nc, "ln3", tokens, out=out)


def kernel(**inputs):
    import concourse.bacc as bacc
    from concourse.bass_utils import run_bass_kernel_spmd

    given = {name: np.ascontiguousarray(value) for name, value in inputs.items()}
    arrays = {**host_delta(given), **delta_constants(), **host_cross(given), **cross_constants(),
              **host_ffn(given), **ffn_constants()}
    nc = bacc.Bacc("TRN2", target_bir_lowering=False, num_devices=1)
    dram = {name: nc.dram_tensor("in_" + name, value.shape, F32, kind="ExternalInput").ap()
            for name, value in arrays.items()}
    alpha_dram = nc.dram_tensor("alpha_rows", (UNITS * VH * NC, P), F32).ap()
    out = nc.dram_tensor("out_0", (TOK, D), F32, kind="ExternalOutput").ap()
    build_program(nc, dram, alpha_dram, out.rearrange("(t p) n -> t p n", p=P))
    result = run_bass_kernel_spmd(nc, [{"in_" + name: value for name, value in arrays.items()}], core_ids=[0])
    return result.results[0]["out_0"].reshape(B, S, D)
```
